# Optimizing a Trainium2 kernel written in Bass

```python
import numpy as np
import jax
import jax.numpy as jnp

def _softmax(x, axis=-1):
    return jax.nn.softmax(x, axis=axis)

def _gelu(x):
    return jax.nn.gelu(x, approximate=True)

def _silu(x):
    return jax.nn.silu(x)

def _sigmoid(x):
    return jax.nn.sigmoid(x)

def _layernorm(x, axis=-1, eps=1e-05):
    m = jnp.mean(x, axis=axis, keepdims=True)
    v = jnp.var(x, axis=axis, keepdims=True)
    return (x - m) / jnp.sqrt(v + eps)

def _scatter_add(tgt, idx, src, axis=0):
    return tgt.at[idx].add(src)

def _segment_sum(src, seg, n):
    return jax.ops.segment_sum(src, seg, n)
kernel_name = 'mk_adj_resnorm_d1_adj_r2_59ffa2'

def setup_inputs(seed: int=0):
    np.random.seed(seed)
    _w = jnp.asarray

    def _rec_inputs():
        import jax
        import jax.numpy as jnp
        _gk = jax.random.key(seed)
        x = -0.0002928 + 1 * jax.random.normal(jax.random.fold_in(_gk, 1), (8, 1024, 256), jnp.float32)
        _a = jax.random.bernoulli(jax.random.fold_in(_gk, 2), 0.0078125, (8, 1024, 1024))
        _a = jnp.logical_or(_a, jnp.swapaxes(_a, -1, -2))
        _a = jnp.logical_or(_a, jnp.eye(1024, dtype=bool))
        adj = _a.astype(jnp.int32)
        return (x, adj)
    x, adj = _rec_inputs()

    def _L0_gnn_setup():
        import jax, jax.numpy as jnp
        import numpy as np
        L = 3
        D = 256
        B, N = (8, 512)
        EPS = 1e-05

        def layernorm(x, gamma, beta):
            mu = jnp.mean(x, axis=-1, keepdims=True)
            var = jnp.var(x, axis=-1, keepdims=True)
            return (x - mu) * jax.lax.rsqrt(var + EPS) * gamma + beta
        key = jax.random.key(seed)
        ks = jax.random.split(key, 12)
        s = 1.0 / np.sqrt(D)
        node_features = jax.random.normal(ks[0], (B, N, D), dtype=jnp.float32)
        adjacency_matrix = jax.random.randint(ks[1], (B, N, N), 0, 2, dtype=jnp.int32)
        return {'node_features': node_features, 'adjacency_matrix': adjacency_matrix, 'attn_w': jax.random.normal(ks[2], (L, 2 * D), dtype=jnp.float32) * (1.0 / np.sqrt(2 * D)), 'attn_b': jax.random.normal(ks[3], (L,), dtype=jnp.float32) * 0.01, 'W1': jax.random.normal(ks[4], (L, D, 4 * D), dtype=jnp.float32) * s, 'b1': jnp.zeros((L, 4 * D), dtype=jnp.float32), 'W2': jax.random.normal(ks[5], (L, 4 * D, D), dtype=jnp.float32) * (1.0 / np.sqrt(4 * D)), 'b2': jnp.zeros((L, D), dtype=jnp.float32), 'g1': jnp.ones((L, D), dtype=jnp.float32), 'beta1': jnp.zeros((L, D), dtype=jnp.float32), 'g2': jnp.ones((L, D), dtype=jnp.float32), 'beta2': jnp.zeros((L, D), dtype=jnp.float32)}
    _L0_gnn_all = _L0_gnn_setup()
    _L0_gnn_in = {k: v for k, v in _L0_gnn_all.items() if k in ('attn_w', 'attn_b', 'W1', 'b1', 'W2', 'b2', 'g1', 'beta1', 'g2', 'beta2')}
    del _L0_gnn_all
    return {'x': x, 'adj': adj, 'L0_gnn_attn_w': _L0_gnn_in['attn_w'], 'L0_gnn_attn_b': _L0_gnn_in['attn_b'], 'L0_gnn_W1': _L0_gnn_in['W1'], 'L0_gnn_b1': _L0_gnn_in['b1'], 'L0_gnn_W2': _L0_gnn_in['W2'], 'L0_gnn_b2': _L0_gnn_in['b2'], 'L0_gnn_g1': _L0_gnn_in['g1'], 'L0_gnn_beta1': _L0_gnn_in['beta1'], 'L0_gnn_g2': _L0_gnn_in['g2'], 'L0_gnn_beta2': _L0_gnn_in['beta2']}

def reference(x, adj, L0_gnn_attn_w, L0_gnn_attn_b, L0_gnn_W1, L0_gnn_b1, L0_gnn_W2, L0_gnn_b2, L0_gnn_g1, L0_gnn_beta1, L0_gnn_g2, L0_gnn_beta2):
    import jax
    import jax.numpy as jnp

    def _L0_gnn_ref(node_features, adjacency_matrix, attn_w, attn_b, W1, b1, W2, b2, g1, beta1, g2, beta2):
        import jax, jax.numpy as jnp
        import numpy as np
        L = 3
        D = 256
        B, N = (8, 512)
        EPS = 1e-05

        def layernorm(x, gamma, beta):
            mu = jnp.mean(x, axis=-1, keepdims=True)
            var = jnp.var(x, axis=-1, keepdims=True)
            return (x - mu) * jax.lax.rsqrt(var + EPS) * gamma + beta
        n = adjacency_matrix.shape[-1]
        mask = adjacency_matrix.astype(jnp.float32) + jnp.eye(n, dtype=jnp.float32) > 0
        x = node_features
        d = x.shape[-1]
        for l in range(attn_w.shape[0]):
            si = x @ attn_w[l, :d]
            sj = x @ attn_w[l, d:]
            scores = si[:, :, None] + sj[:, None, :] + attn_b[l]
            scores = jnp.where(scores >= 0, scores, 0.2 * scores)
            scores = jnp.where(mask, scores, -jnp.inf)
            attn = jax.nn.softmax(scores, axis=-1)
            agg = jnp.einsum('bij,bjd->bid', attn, x)
            h = layernorm(x + agg, g1[l], beta1[l])
            ff = jax.nn.gelu(h @ W1[l] + b1[l], approximate=False) @ W2[l] + b2[l]
            x = layernorm(h + ff, g2[l], beta2[l])
        return x
    x = _layernorm(x + _L0_gnn_ref(x, adj, L0_gnn_attn_w, L0_gnn_attn_b, L0_gnn_W1, L0_gnn_b1, L0_gnn_W2, L0_gnn_b2, L0_gnn_g1, L0_gnn_beta1, L0_gnn_g2, L0_gnn_beta2), axis=-1)
    return x

_drawn_inputs = setup_inputs


def setup_inputs(seed=0):
    import zlib

    import numpy as np

    out = dict(_drawn_inputs(seed))
    spreads = {'L0_gnn_b1': (0.0, 0.1),
     'L0_gnn_b2': (0.0, 0.1),
     'L0_gnn_g1': (1.0, 0.2),
     'L0_gnn_beta1': (0.0, 0.1),
     'L0_gnn_g2': (1.0, 0.2),
     'L0_gnn_beta2': (0.0, 0.1)}
    factors = {'L0_gnn_attn_b': 64.0}
    for name, (base, spread) in spreads.items():
        noise = np.random.default_rng([zlib.crc32(name.encode()), seed]).standard_normal(out[name].shape)
        drawn = base * np.exp(spread * noise) if base else spread * noise
        out[name] = jnp.asarray(drawn.astype(out[name].dtype))
    for name, factor in factors.items():
        out[name] = (out[name] * factor).astype(out[name].dtype)
    return out
```

```python
import concourse.bass as bass
from concourse import mybir
from contextlib import ExitStack

P = 128
B, N, D = 8, 1024, 256
L = 3
FF = 4 * D
NT = N // P
KD = D // P
NC = FF // P
HALF = N // 2
HT = HALF // P
NQ = NT // 2
PAIRS = B // 2
STEPS = L * 2 * 2
DX = D + 2
EPS = 1e-5
SLOPE = 0.2


def gnn_kernel(nc, x_d, adj_d, attn_w, attn_b, W1, b1, W2, b2, g1, beta1, g2, beta2, out_d):
    f32, f32r = mybir.dt.float32, mybir.dt.float32r
    bf16, u8, i32 = mybir.dt.bfloat16, mybir.dt.uint8, mybir.dt.int32
    ALU, ACT, AX = mybir.AluOpType, mybir.ActivationFunctionType, mybir.AxisListType

    ctx = ExitStack()
    with ctx:
        def sb(name, shape, dt):
            return ctx.enter_context(nc.sbuf_tensor(name, shape, dt))

        def sem(name):
            return ctx.enter_context(nc.semaphore(name))

        w_hi = sb("w_hi", [P, NC, 2 * D], f32r)
        w_lo = sb("w_lo", [P, NC, 2 * D], f32r)
        w_stage = sb("w_stage", [P, 2 * D], f32)
        x = [sb(f"x{b}", [P, NT, D], f32) for b in range(2)]
        x_hi = [sb(f"x_hi{b}", [P, NT, DX], f32r) for b in range(2)]
        x_lo = [sb(f"x_lo{b}", [P, NT, DX], f32r) for b in range(2)]
        mask_src = [sb(f"mask_src{b}", [P, NT, N], u8) for b in range(2)]
        mask_dst = [sb(f"mask_dst{b}", [P, NT, N], u8) for b in range(2)]
        s = [sb(f"s{b}", [P, NT, 3], f32) for b in range(2)]
        adj_stage = sb("adj_stage", [P, N], i32)
        mask_bf = sb("mask_bf", [P, N], bf16)
        sj_row = sb("sj_row", [P, N], f32)
        r_rows = sb("r_rows", [P, 2, HALF], f32)
        e1 = sb("e1", [P, 2, 2, HALF], f32)
        e2 = sb("e2", [P, 2, HALF], f32)
        p_hi = sb("p_hi", [P, 2, 2, HALF], f32r)
        p_lo = sb("p_lo", [P, 2, 2, HALF], f32r)
        y1 = sb("y1", [P, HT, D], f32)
        hT = sb("hT", [P, 2, KD, HALF], f32)
        hT_hi = sb("hT_hi", [P, KD, HALF], f32r)
        hT_lo = sb("hT_lo", [P, KD, HALF], f32r)
        g = sb("g", [P, 2, HALF], f32)
        g_hi = sb("g_hi", [P, 2, HALF], f32r)
        g_lo = sb("g_lo", [P, 2, HALF], f32r)
        n2 = sb("n2", [P, HT, D], f32)
        w_row = sb("w_row", [P, 2, D], f32)
        g2_row = sb("g2_row", [P, D], f32)
        beta2_row = sb("beta2_row", [P, D], f32)
        b1_col = sb("b1_col", [P, L, NC], f32)
        b2_col = sb("b2_col", [P, L, KD], f32)
        g1_col = sb("g1_col", [P, L, KD], f32)
        beta1_col = sb("beta1_col", [P, L, KD], f32)
        attn_b_col = sb("attn_b_col", [P, L], f32)
        ident = sb("ident", [P, P], f32)
        ident_bf = sb("ident_bf", [P, P], bf16)
        eye = sb("eye", [P, P], i32)
        unused = sb("unused", [P, N], bf16)
        bn1 = sb("bn1", [P, HT, 6], f32)
        mv1 = sb("mv1", [P, HT, 2], f32)
        rstd1 = sb("rstd1", [P, HT], f32)
        bn2 = sb("bn2", [P, HT, 6], f32)
        mv2 = sb("mv2", [P, HT, 2], f32)
        rstd2 = sb("rstd2", [P, HT], f32)
        power = sb("power", [P, HT], f32)
        gate_cell = sb("gate_cell", [P, 1], f32)
        eps = sb("eps", [P, HT], f32)
        r_sum = sb("r_sum", [P, HT], f32)
        sj_min = sb("sj_min", [P, 1], f32)
        sj_max = sb("sj_max", [P, HT], f32)
        z0 = sb("z0", [P, HT], f32)
        zm = sb("zm", [P, HT], f32)
        row_max = sb("row_max", [P, HT], f32)
        r_col = sb("r_col", [P, 2, HT], f32)

        agg = ctx.enter_context(nc.psum_tensor("agg", [P, 4, 512], f32))
        ff1 = ctx.enter_context(nc.psum_tensor("ff1", [P, 2, 512], f32))
        ff2 = ctx.enter_context(nc.psum_tensor("ff2", [P, 2, 512], f32))

        params_in = sem("params_in")
        rows_in = sem("rows_in")
        x_in = sem("x_in")
        x0_in = sem("x0_in")
        adj_in = sem("adj_in")
        w_in = sem("w_in")
        out_done = sem("out_done")
        consts = sem("consts")
        diag_added = sem("diag_added")
        mask_ready = sem("mask_ready")
        dst_ready = sem("dst_ready")
        mask_turned = sem("mask_turned")
        src_ready = sem("src_ready")
        w_split_hi = sem("w_split_hi")
        w_split = sem("w_split")
        x_hi_ready = sem("x_hi_ready")
        x_lo_ready = sem("x_lo_ready")
        s_ready = sem("s_ready")
        sj_turned = sem("sj_turned")
        sj_copied = sem("sj_copied")
        cols_ready = sem("cols_ready")
        r_turned = sem("r_turned")
        r_copied = sem("r_copied")
        exps = sem("exps")
        maxed = sem("maxed")
        p_hi_ready = sem("p_hi_ready")
        p_lo_ready = sem("p_lo_ready")
        agg_done = sem("agg_done")
        agg_read = sem("agg_read")
        stats1 = sem("stats1")
        rstd1_ready = sem("rstd1_ready")
        n1_ready = sem("n1_ready")
        n1_turned = sem("n1_turned")
        hT_ready = sem("hT_ready")
        hT_hi_ready = sem("hT_hi_ready")
        hT_lo_ready = sem("hT_lo_ready")
        ff1_done = sem("ff1_done")
        gelus = sem("gelus")
        g_hi_ready = sem("g_hi_ready")
        g_lo_ready = sem("g_lo_ready")
        ff2_done = sem("ff2_done")
        y2_ready = sem("y2_ready")
        y2_turned = sem("y2_turned")
        stats2 = sem("stats2")
        rstd2_ready = sem("rstd2_ready")
        n2_ready = sem("n2_ready")
        x_ready = sem("x_ready")
        stats3 = sem("stats3")
        rstd3_ready = sem("rstd3_ready")
        out_ready = sem("out_ready")
        dve_link = sem("dve_link")
        pool_link = sem("pool_link")

        class Links:
            def __init__(self, eng, own, per_round):
                self.eng, self.own, self.per_round, self.n, self.round = eng, own, per_round, 0, None

            def after(self, ins):
                self.n += 1
                ins.then_inc(self.own, 1)
                self.eng.wait_ge(self.own, self.n if self.round is None
                                 else self.round * self.per_round + self.n)

        def masks_before(i, k):
            return 16 if i is None else i * 16 + (16 + 4 * (k - 8))

        def x_count(i, kk):
            if i is None:
                return kk // 2 + 1
            return i * 10 + {1: 2, 2: 4, 3: 6, 4: 8, 5: 10, 6: 11}[kk // 2]

        def feed_slot(k):
            return (k // 2) % 2, k % 2, k // 4

        def attend_slot(k):
            return (k // 2) % 2, k % 2, (k // 4) % L

        block = ctx.enter_context(nc.Block())

        @block.sync
        def _(sp):
            def load_rows(score_layer, norm_layer):
                sp.dma_start(w_row[:, :, :], attn_w[score_layer, :].rearrange("(a c) -> a c", a=2)
                             .partition_broadcast(P)).then_inc(rows_in, 16)
                sp.dma_start(g2_row[:, :], g2[norm_layer, :].partition_broadcast(P)).then_inc(rows_in, 16)
                sp.dma_start(beta2_row[:, :], beta2[norm_layer, :].partition_broadcast(P)).then_inc(rows_in, 16)

            def load_chunk(layer, c, first, n_split):
                if not first:
                    sp.wait_ge(w_split, n_split)
                sp.dma_start(w_stage[:, 0:D].rearrange("p (k n) -> p k n", k=KD),
                             W1[layer, :, c * P:(c + 1) * P].rearrange("(k p) n -> p k n", p=P)).then_inc(w_in, 16)
                sp.dma_start(w_stage[:, D:2 * D], W2[layer, c * P:(c + 1) * P, :]).then_inc(w_in, 16)

            def load_adj(batch, it, first, n_mask):
                if not first:
                    sp.wait_ge(mask_ready, n_mask)
                sp.dma_start(adj_stage[:, :], adj_d[batch, it * P:(it + 1) * P, :]).then_inc(adj_in, 16)

            load_rows(0, 0)
            sp.dma_start(x[0][:, :, :], x_d[0, :, :].rearrange("(t p) d -> p t d", p=P)).then_inc(x_in, 16)
            load_adj(0, 0, True, 0)
            for dst, src in ((b1_col, b1), (b2_col, b2), (g1_col, g1), (beta1_col, beta1)):
                sp.dma_start(dst[:, :, :], src.rearrange("l (c p) -> p l c", p=P),
                             allow_slow_non_contiguous=True).then_inc(params_in, 16)
            sp.dma_start(attn_b_col[:, :], attn_b.partition_broadcast(P)).then_inc(params_in, 16)
            for m in range(1, 2 * NT):
                load_adj(m // NT, m % NT, False, m)
                if m == 1:
                    sp.wait_ge(x_in, 16)
                    sp.dma_start(x[1][:, :, :], x_d[1, :, :].rearrange("(t p) d -> p t d", p=P)).then_inc(x_in, 16)
                if m % 2 == 0:
                    load_chunk(0, m // 2 - 1, m == 2, m // 2 - 1)
            load_chunk(0, NC - 1, False, NC - 1)
            sp.wait_ge(s_ready, 2)
            load_rows(1, 0)

            with sp.Fori(0, PAIRS) as i:
                nxt = (i + 1) % PAIRS
                for k in range(STEPS):
                    t = i * STEPS + k
                    b, h, layer = feed_slot(k)
                    if k >= 8:
                        sp.wait_ge(n1_turned, t + 2)
                        sp.dma_start(y1[:, :, :], x_d[i * 2 + b, h * HALF:(h + 1) * HALF, :]
                                     .rearrange("(t p) d -> p t d", p=P)).then_inc(x0_in, 16)
                    for q in range(NQ):
                        if k >= 8:
                            load_adj(nxt * 2 + (k - 8) // 2, (k % 2) * 4 + q, False, masks_before(i, k) + q)
                        if k == 9 and q == 0 or k == 11 and q == 0:
                            sp.dma_start(x[b][:, :, :], x_d[nxt * 2 + b, :, :]
                                         .rearrange("(t p) d -> p t d", p=P)).then_inc(x_in, 16)
                        if k % 4 == 3:
                            for c in (2 * q, 2 * q + 1):
                                n_split = i * (L * NC) + (layer + 1) * NC + c
                                if c == 0:
                                    sp.wait_ge(ff2_done, t * NC + NC)
                                load_chunk((layer + 1) % L, c, c == 0, n_split)
                    if k >= 8:
                        sp.wait_ge(out_ready, i * 4 + k - 7)
                        sp.dma_start(out_d[i * 2 + b, h * HALF:(h + 1) * HALF, :]
                                     .rearrange("(t p) d -> p t d", p=P), n2[:, :, :]).then_inc(out_done, 16)
                    if k % 4 == 3:
                        sp.wait_ge(s_ready, i * 10 + {3: 6, 7: 10, 11: 12}[k])
                        load_rows({3: 2, 7: 0, 11: 1}[k], (layer + 1) % L)
            sp.wait_ge(out_done, 16 * B * 2)
            sp.wait_ge(rows_in, 48 * (2 + 3 * PAIRS))

        @block.gpsimd
        def _(pool):
            links = Links(pool, pool_link, 3 * STEPS + 4)
            eng = nc.gpsimd

            def split_lo(dst, value, hi, ready):
                eng.tensor_tensor(dst, value, hi.bitcast(f32), ALU.subtract).then_inc(ready, 1)

            def mask_tile(it, n_in):
                pool.wait_ge(adj_in, n_in * 16)
                d = adj_stage[:, it * P:(it + 1) * P]
                eng.tensor_tensor(d, d, eye[:, :], ALU.add).then_inc(diag_added, 1)

            def inv_std(mv, dst, stats, n_stats, ready):
                pool.wait_ge(stats, n_stats)
                links.after(eng.tensor_tensor(dst[:, :], mv[:, :, 1], eps[:, :], ALU.add))
                eng.tensor_tensor(dst[:, :], dst[:, :], power[:, :], ALU.pow).then_inc(ready, 1)

            def new_batch_lo(b, n):
                pool.wait_ge(x_hi_ready, n)
                split_lo(x_lo[b][:, :, 0:D], x[b][:, :, :], x_hi[b][:, :, 0:D], x_lo_ready)

            def chunk_lo(c, n):
                pool.wait_ge(w_split_hi, n)
                split_lo(w_lo[:, c, :], w_stage[:, :], w_hi[:, c, :], w_split)

            def p_lo_pair(a, q):
                pool.wait_ge(p_hi_ready, a * NQ + q + 1)
                split_lo(p_lo[:, q % 2], e1[:, q % 2], p_hi[:, q % 2], p_lo_ready)

            eng.memset(ident[:, :], 0.0).then_inc(pool_link, 1)
            eng.memset(eye[:, :], 0).then_inc(pool_link, 1)
            eng.memset(power[:, :], -0.5)
            eng.memset(eps[:, :], EPS)
            for b in range(2):
                eng.memset(x_hi[b][:, :, D:D + 1].bitcast(f32), 1.0)
                eng.memset(x_hi[b][:, :, D + 1:DX].bitcast(f32), 0.0)
                eng.memset(x_lo[b][:, :, D:DX].bitcast(f32), 0.0)
            pool.wait_ge(pool_link, 2)
            eng.affine_select(out=ident[:, :], in_=ident[:, :], compare_op=ALU.not_equal, fill=1.0, base=0,
                              pattern=[[-1, P]], channel_multiplier=1).then_inc(pool_link, 1)
            pool.wait_ge(pool_link, 3)
            eng.tensor_copy(eye[:, :], ident[:, :]).then_inc(pool_link, 1)
            eng.tensor_copy(ident_bf[:, :], ident[:, :]).then_inc(consts, 1)
            pool.wait_ge(pool_link, 4)
            links.n = 4
            for m in range(2 * NT):
                mask_tile(m % NT, m + 1)
                if m == 0:
                    new_batch_lo(0, 1)
                if m == 2:
                    new_batch_lo(1, 2)
                if m >= 2 and m % 2 == 0:
                    chunk_lo(m // 2 - 1, m // 2)
            chunk_lo(NC - 1, NC)
            for q in range(NQ):
                p_lo_pair(0, q)
            inv_std(mv1, rstd1, stats1, 1, rstd1_ready)
            pool.wait_ge(hT_hi_ready, 1)
            split_lo(hT_lo[:, :, :], hT[:, 0], hT_hi[:, :, :], hT_lo_ready)
            for q in range(NQ):
                p_lo_pair(1, q)
            n_ahead = links.n

            with pool.Fori(0, PAIRS) as i:
                links.round, links.n = i, n_ahead
                for k in range(STEPS):
                    t = i * STEPS + k
                    b, h, layer = feed_slot(k)
                    rows = slice(h * HT, (h + 1) * HT)
                    for c in range(NC):
                        pool.wait_ge(g_hi_ready, t * NC + c + 1)
                        split_lo(g_lo[:, c % 2], g[:, c % 2], g_hi[:, c % 2], g_lo_ready)
                        if c == 0:
                            inv_std(mv1, rstd1, stats1, t + 2, rstd1_ready)
                    pool.wait_ge(hT_hi_ready, t + 2)
                    split_lo(hT_lo[:, :, :], hT[:, (k + 1) % 2], hT_hi[:, :, :], hT_lo_ready)
                    for q in range(NQ):
                        if k >= 8:
                            mask_tile((k % 2) * 4 + q, masks_before(i, k) + q + 1)
                        p_lo_pair(t + 2, q)
                        if k % 4 == 3:
                            for c in (2 * q, 2 * q + 1):
                                chunk_lo(c, i * (L * NC) + (layer + 1) * NC + c + 1)
                        if q == 2:
                            inv_std(mv2, rstd2, stats2, t + 1, rstd2_ready)
                    pool.wait_ge(n2_ready, t + 2)
                    if k % 4 == 0:
                        pool.wait_ge(rows_in, (i * 3 + 2 + layer) * 48)
                    links.after(eng.tensor_tensor(n2[:, :, :], n2[:, :, :],
                                                  g2_row[:, :].unsqueeze(1).broadcast_to([P, HT, D]), ALU.mult))
                    dst = x[b][:, rows, :] if layer < L - 1 else n2[:, :, :]
                    eng.tensor_tensor(dst, n2[:, :, :], beta2_row[:, :].unsqueeze(1).broadcast_to([P, HT, D]),
                                      ALU.add).then_inc(x_ready, 1)
                    if layer < L - 1:
                        pool.wait_ge(x_hi_ready, i * 10 + k + 3)
                        split_lo(x_lo[b][:, rows, 0:D], x[b][:, rows, :], x_hi[b][:, rows, 0:D], x_lo_ready)
                    else:
                        inv_std(mv2, rstd2, stats3, i * 4 + k - 7, rstd3_ready)
                    if k in (9, 11):
                        new_batch_lo(b, i * 10 + {9: 11, 11: 12}[k])
                assert links.n - n_ahead == links.per_round

        @block.scalar
        def _(act):
            eng = nc.scalar

            def mask_tile(b, it, n):
                act.wait_ge(mask_ready, n)
                eng.activation(mask_dst[b][:, it, :], mask_bf[:, :], ACT.Copy).then_inc(dst_ready, 1)
                act.wait_ge(mask_turned, n)
                eng.activation(mask_src[b][:, :, it * P:(it + 1) * P],
                               ff2[:, it % 2, :].bitcast(bf16).rearrange("p (j i) -> p j i", j=NT),
                               ACT.Copy).then_inc(src_ready, 1)

            def sj_copy(n):
                act.wait_ge(sj_turned, n)
                eng.activation(sj_row[:, :].rearrange("p (a n) -> p a n", a=2), agg[:, 2:4, :],
                               ACT.Copy).then_inc(sj_copied, 1)

            def r_copy(a):
                act.wait_ge(r_turned, a + 1)
                eng.activation(r_rows[:, :, :], agg[:, 2:4, :], ACT.Copy).then_inc(r_copied, 1)

            def hT_copy(a, buf, layer):
                act.wait_ge(n1_turned, a + 1)
                for kd in range(KD):
                    ins = eng.activation(hT[:, buf, kd, :], agg[:, kd, :], ACT.Identity,
                                         bias=beta1_col[:, layer, kd:kd + 1], scale=g1_col[:, layer, kd:kd + 1])
                ins.then_inc(hT_ready, 1)

            def exp_pair(b, a, q, e1_free, e2_free):
                if e1_free:
                    act.wait_ge(p_lo_ready, a * NQ + q - 1)
                if e2_free:
                    act.wait_ge(maxed, a * NQ + q)
                if q == 0:
                    act.wait_ge(r_copied, a + 1)
                for j in range(2):
                    eng.activation(e1[:, q % 2, j, :], r_rows[:, 0, :], ACT.Exp,
                                   bias=s[b][:, 2 * q + j, 1:2], scale=1.0)
                for j in range(2):
                    ins = eng.activation(e2[:, j, :], r_rows[:, 1, :], ACT.Exp,
                                         bias=s[b][:, 2 * q + j, 2:3], scale=1.0)
                ins.then_inc(exps, 1)

            act.wait_ge(x_in, 16)
            eng.activation(x_hi[0][:, :, 0:D], x[0][:, :, :], ACT.Copy).then_inc(x_hi_ready, 1)
            for m in range(2 * NT):
                mask_tile(m // NT, m % NT, m + 1)
                if m == 1:
                    act.wait_ge(x_in, 32)
                    eng.activation(x_hi[1][:, :, 0:D], x[1][:, :, :], ACT.Copy).then_inc(x_hi_ready, 1)
            act.wait_ge(params_in, 16 * 5)
            sj_copy(1)
            r_copy(0)
            for q in range(NQ):
                exp_pair(0, 0, q, q >= 2, q >= 1)
            hT_copy(0, 0, 0)
            r_copy(1)
            for q in range(NQ):
                exp_pair(0, 1, q, True, True)

            with act.Fori(0, PAIRS) as i:
                for k in range(STEPS):
                    t = i * STEPS + k
                    b, h, layer = feed_slot(k)
                    ab, ah, _l = attend_slot(k + 2)
                    for c in range(NC):
                        act.wait_ge(ff1_done, t * NC + c + 1)
                        if c >= 2:
                            act.wait_ge(g_lo_ready, t * NC + c - 1)
                        eng.activation(g[:, c % 2, :], ff1[:, c % 2, :], ACT.Gelu,
                                       bias=b1_col[:, layer, c:c + 1], scale=1.0).then_inc(gelus, 1)
                        if c == 1 and ah == 0:
                            sj_copy(i * (STEPS // 2) + (k + 2) // 2 + 1)
                        if c == 4:
                            hT_copy(t + 1, (k + 1) % 2, ((k + 1) // 4) % L)
                    r_copy(t + 2)
                    for q in range(NQ):
                        exp_pair(ab, t + 2, q, True, True)
                        if k >= 8 and q >= 1:
                            mask_tile((k - 8) // 2, (k % 2) * 4 + q - 1, masks_before(i, k) + q)
                    if k >= 8:
                        mask_tile((k - 8) // 2, (k % 2) * 4 + NQ - 1, masks_before(i, k) + NQ)
                    if layer < L - 1:
                        rows = slice(h * HT, (h + 1) * HT)
                        act.wait_ge(x_ready, t + 1)
                        eng.activation(x_hi[b][:, rows, 0:D], x[b][:, rows, :], ACT.Copy).then_inc(x_hi_ready, 1)
                    if k in (9, 11):
                        act.wait_ge(x_in, (i * 2 + {9: 3, 11: 4}[k]) * 16)
                        eng.activation(x_hi[b][:, :, 0:D], x[b][:, :, :], ACT.Copy).then_inc(x_hi_ready, 1)

        @block.vector
        def _(dve):
            eng = nc.vector
            links = Links(dve, dve_link, STEPS * (3 + NQ + HT + 3) + STEPS // 2 * 2 + (L - 1) * 4 * 2 * HT
                          + 4 * 2 + 2 * 2 * NT)

            def gate():
                eng.memset(gate_cell[:, :], 0.0)

            def mask_tile(n, first):
                dve.wait_ge(diag_added, n)
                if not first:
                    dve.wait_ge(dst_ready, n - 1)
                    dve.wait_ge(mask_turned, n - 1)
                eng.tensor_scalar(mask_bf[:, :], adj_stage[:, :], 0.0, None, ALU.is_gt).then_inc(mask_ready, 1)

            def scores(b, tiles):
                for it in tiles:
                    for side in range(2):
                        links.after(eng.tensor_tensor_reduce(
                            out=unused[:, 0:D], in0=x[b][:, it, :], in1=w_row[:, side, :], scale=1.0, scalar=0.0,
                            op0=ALU.mult, op1=ALU.add, accum_out=s[b][:, it, side:side + 1]))
                sl = slice(tiles[0], tiles[-1] + 1)
                eng.tensor_scalar(s[b][:, sl, 2], s[b][:, sl, 1], SLOPE, None, ALU.mult).then_inc(s_ready, 1)

            def chunk_hi(c, n):
                dve.wait_ge(w_in, n * 32)
                eng.tensor_copy(w_hi[:, c, :], w_stage[:, :]).then_inc(w_split_hi, 1)

            def source_min(n):
                dve.wait_ge(sj_copied, n)
                links.after(eng.tensor_reduce(out=sj_min[:, :], in_=sj_row[:, :], axis=AX.X, op=ALU.min))
                links.after(eng.tensor_scalar(sj_row[:, :], sj_row[:, :], sj_min[:, :], None, ALU.subtract))

            def row_maxima(b, its):
                for it in its:
                    links.after(eng.tensor_tensor_reduce(
                        out=unused[:, :], in0=sj_row[:, :], in1=mask_dst[b][:, it, :], scale=1.0, scalar=0.0,
                        op0=ALU.mult, op1=ALU.max, accum_out=sj_max[:, it % HT:it % HT + 1]))
                    gate()

            def shift_columns(b, h, layer):
                si = s[b][:, h * HT:(h + 1) * HT, 0]
                links.after(eng.tensor_scalar(z0[:, :], si, attn_b_col[:, layer:layer + 1], None, ALU.add))
                links.after(eng.scalar_tensor_tensor(out=zm[:, :], in0=sj_max[:, :], scalar=sj_min[:, :],
                                                     in1=z0[:, :], op0=ALU.add, op1=ALU.add))
                links.after(eng.scalar_tensor_tensor(out=row_max[:, :], in0=zm[:, :], scalar=SLOPE,
                                                     in1=zm[:, :], op0=ALU.mult, op1=ALU.max))
                eng.tensor_tensor(r_col[:, 0, :], z0[:, :], row_max[:, :], ALU.subtract)
                eng.scalar_tensor_tensor(out=r_col[:, 1, :], in0=z0[:, :], scalar=SLOPE, in1=row_max[:, :],
                                         op0=ALU.mult, op1=ALU.subtract).then_inc(cols_ready, 1)

            def mask_pair(b, h, a, q, p_free):
                dve.wait_ge(exps, a * NQ + q + 1)
                e = e1[:, q % 2]
                ins = eng.tensor_tensor(e, e, e2[:, :, :], ALU.max)
                ins.then_inc(maxed, 1)
                dve.wait_ge(maxed, a * NQ + q + 1)
                links.after(eng.tensor_tensor(e, e, mask_src[b][:, 2 * q:2 * q + 2, h * HALF:(h + 1) * HALF], ALU.min))
                if p_free:
                    dve.wait_ge(agg_done, a * NQ + q - 1)
                eng.tensor_copy(p_hi[:, q % 2], e).then_inc(p_hi_ready, 1)

            def residual1(b, h, a):
                dve.wait_ge(agg_done, a * NQ + NQ)
                for it in range(HT):
                    ins = eng.reciprocal(r_sum[:, it:it + 1], agg[:, it, D:D + 1])
                links.after(ins)
                for it in range(HT):
                    ins = eng.scalar_tensor_tensor(out=y1[:, it, :], in0=agg[:, it, 0:D], scalar=r_sum[:, it:it + 1],
                                                   in1=x[b][:, h * HT + it, :], op0=ALU.mult, op1=ALU.add)
                ins.then_inc(agg_read, 1)
                dve.wait_ge(agg_read, a + 1)

            def mean_var(src, bn, mv, ready, n):
                for it in range(HT):
                    ins = eng.bn_stats(bn[:, it, :], src(it))
                links.after(ins)
                gate()
                for it in range(HT):
                    ins = eng.bn_aggr(mv[:, it, :], bn[:, it, :])
                ins.then_inc(ready, 1)

            def normalize(dst, src, mv, rstd, ready, n, n_ready=1):
                dve.wait_ge(ready, n)
                for it in range(HT):
                    ins = eng.tensor_scalar(dst[:, it, :], src(it), mv[:, it, 0:1], rstd[:, it:it + 1],
                                            ALU.subtract, ALU.mult)
                return ins

            def hT_split(a, buf):
                dve.wait_ge(hT_ready, a + 1)
                eng.tensor_copy(hT_hi[:, :, :], hT[:, buf]).then_inc(hT_hi_ready, 1)

            eng.memset(bn1[:, 0, :], 0.0).then_inc(y2_ready, 1)
            eng.memset(bn2[:, 0, :], 0.0).then_inc(n2_ready, 1)
            dve.wait_ge(rows_in, 48)
            for m in range(2 * NT):
                mask_tile(m + 1, m == 0)
                if m == 0:
                    dve.wait_ge(x_in, 16)
                    scores(0, range(NT))
                if m == 2:
                    dve.wait_ge(x_in, 32)
                    scores(1, range(NT))
                if m >= 2 and m % 2 == 0:
                    chunk_hi(m // 2 - 1, m // 2)
            chunk_hi(NC - 1, NC)
            dve.wait_ge(params_in, 16 * 5)
            dve.wait_ge(dst_ready, 2 * NT)
            dve.wait_ge(src_ready, 2 * NT)
            source_min(1)
            row_maxima(0, range(HT))
            shift_columns(0, 0, 0)
            for q in range(NQ):
                mask_pair(0, 0, 0, q, q >= 2)
            residual1(0, 0, 0)
            mean_var(lambda it: y1[:, it, :], bn1, mv1, stats1, 1)
            normalize(y1, lambda it: y1[:, it, :], mv1, rstd1, rstd1_ready, 1).then_inc(n1_ready, 1)
            hT_split(0, 0)
            row_maxima(0, range(HT, 2 * HT))
            shift_columns(0, 1, 0)
            for q in range(NQ):
                mask_pair(0, 1, 1, q, True)
            n_ahead = links.n

            with dve.Fori(0, PAIRS) as i:
                links.round, links.n = i, n_ahead
                for k in range(STEPS):
                    t = i * STEPS + k
                    b, h, layer = feed_slot(k)
                    ab, ah, al = attend_slot(k + 2)
                    nb, nh, _l = attend_slot(k + 1)

                    def gelu_hi(c):
                        dve.wait_ge(gelus, t * NC + c + 1)
                        if c >= 2:
                            dve.wait_ge(ff2_done, t * NC + c - 1)
                        eng.tensor_copy(g_hi[:, c % 2], g[:, c % 2]).then_inc(g_hi_ready, 1)

                    residual1(nb, nh, t + 1)
                    gelu_hi(0)
                    mean_var(lambda it: y1[:, it, :], bn1, mv1, stats1, t + 2)
                    gelu_hi(1)
                    normalize(y1, lambda it: y1[:, it, :], mv1, rstd1, rstd1_ready, t + 2).then_inc(n1_ready, 1)
                    gelu_hi(2)
                    if ah == 0:
                        if k + 2 == STEPS or k + 2 == 2:
                            if k + 2 == STEPS:
                                dve.wait_ge(dst_ready, masks_before(i, 10))
                            else:
                                dve.wait_ge(dst_ready, masks_before(i, 8))
                        source_min(i * (STEPS // 2) + (k + 2) // 2 + 1)
                    gelu_hi(3)
                    row_maxima(ab, range(ah * HT, ah * HT + 2))
                    gelu_hi(4)
                    row_maxima(ab, range(ah * HT + 2, ah * HT + 4))
                    shift_columns(ab, ah, al)
                    for c in range(5, NC):
                        gelu_hi(c)
                    dve.wait_ge(ff1_done, t * NC + NC)
                    hT_split(t + 1, (k + 1) % 2)

                    for q in range(NQ):
                        mask_pair(ab, ah, t + 2, q, True)
                        if k % 4 == 3:
                            for c in (2 * q, 2 * q + 1):
                                chunk_hi(c, i * (L * NC) + (layer + 1) * NC + c + 1)
                        if q == 0:
                            dve.wait_ge(ff2_done, t * NC + NC)
                            for kd in range(KD):
                                ins = eng.scalar_tensor_tensor(
                                    out=hT[:, k % 2, kd, :], in0=ff2[:, kd, :], scalar=b2_col[:, layer, kd:kd + 1],
                                    in1=hT[:, k % 2, kd, :], op0=ALU.add, op1=ALU.add)
                            ins.then_inc(y2_ready, 1)
                        if k >= 8:
                            mask_tile(masks_before(i, k) + q + 1, False)
                        if q == 2:
                            dve.wait_ge(y2_turned, t + 1)
                            y2 = lambda it: ff1[:, it // 2, (it % 2) * D:(it % 2 + 1) * D]
                            mean_var(y2, bn2, mv2, stats2, t + 1)
                    if k > 8:
                        dve.wait_ge(out_done, (i * 4 + k - 8) * 16)
                    normalize(n2, y2, mv2, rstd2, rstd2_ready, t + 1).then_inc(n2_ready, 1)
                    dve.wait_ge(x_ready, t + 1)
                    if layer < L - 1:
                        if k % 4 == 0:
                            dve.wait_ge(rows_in, (i * 3 + 2 + layer) * 48)
                        scores(b, range(h * HT, (h + 1) * HT))
                    else:
                        dve.wait_ge(x0_in, (i * 4 + k - 7) * 16)
                        links.after(eng.tensor_tensor(n2[:, :, :], n2[:, :, :], y1[:, :, :], ALU.add))
                        mean_var(lambda it: n2[:, it, :], bn2, mv2, stats3, 0)
                        normalize(n2, lambda it: n2[:, it, :], mv2, rstd2, rstd3_ready,
                                  i * 4 + k - 7).then_inc(out_ready, 1)
                    if k in (9, 11):
                        dve.wait_ge(x_in, (i * 2 + {9: 3, 11: 4}[k]) * 16)
                        dve.wait_ge(rows_in, (i * 3 + 4) * 48)
                        scores(b, range(NT))
                    if k == 11:
                        dve.wait_ge(out_done, (i * 4 + 4) * 16)
                assert links.n - n_ahead == links.per_round

        @block.tensor
        def _(pe):
            eng = nc.tensor

            def mask_tile(it, n, first):
                pe.wait_ge(mask_ready, n)
                if not first:
                    pe.wait_ge(src_ready, n - 2)
                bank = ff2[:, it % 2, :].bitcast(bf16)
                for j in range(NT):
                    ins = eng.transpose(bank[:, j * P:(j + 1) * P], mask_bf[:, j * P:(j + 1) * P], ident_bf[:, :])
                ins.then_inc(mask_turned, 1)

            def sj_turn(b, n_s, n_agg):
                pe.wait_ge(s_ready, n_s)
                if n_agg is not None:
                    pe.wait_ge(agg_read, n_agg)
                for j in range(NT):
                    ins = eng.transpose(agg[:, 2 + j // 4, (j % 4) * P:(j % 4 + 1) * P],
                                        s[b][:, j, 1:2].to_broadcast([P, P]), ident[:, :])
                ins.then_inc(sj_turned, 1)

            def r_turn(a, n_sj, n_agg):
                pe.wait_ge(cols_ready, a + 1)
                pe.wait_ge(sj_copied, n_sj)
                if n_agg is not None:
                    pe.wait_ge(agg_read, n_agg)
                for r in range(2):
                    for it in range(HT):
                        ins = eng.transpose(agg[:, 2 + r, it * P:(it + 1) * P],
                                            r_col[:, r, it:it + 1].to_broadcast([P, P]), ident[:, :])
                ins.then_inc(r_turned, 1)

            def aggregate(b, a, q, n_x, first_step):
                if q == 0:
                    pe.wait_ge(r_copied, a + 1)
                    pe.wait_ge(x_lo_ready, n_x)
                    if not first_step:
                        pe.wait_ge(hT_ready, a)
                pe.wait_ge(p_lo_ready, a * NQ + q + 1)
                for j in range(2):
                    jt = 2 * q + j
                    for it in range(HT):
                        hi = p_hi[:, q % 2, j, it * P:(it + 1) * P]
                        lo = p_lo[:, q % 2, j, it * P:(it + 1) * P]
                        bank = agg[:, it, 0:DX]
                        eng.matmul(bank, hi, x_lo[b][:, jt, :], start=(jt == 0), stop=False)
                        eng.matmul(bank, hi, x_hi[b][:, jt, :], start=False, stop=False)
                        ins = eng.matmul(bank, lo, x_hi[b][:, jt, :], start=False, stop=(jt == NT - 1))
                ins.then_inc(agg_done, 1)

            def n1_turn(a):
                pe.wait_ge(n1_ready, a + 1)
                for kd in range(KD):
                    for it in range(HT):
                        ins = eng.transpose(agg[:, kd, it * P:(it + 1) * P], y1[:, it, kd * P:(kd + 1) * P], ident[:, :])
                ins.then_inc(n1_turned, 1)

            def hidden(t, c):
                if c == 0:
                    pe.wait_ge(n2_ready, t + 1)
                    pe.wait_ge(hT_lo_ready, t + 1)
                if c >= 2:
                    pe.wait_ge(gelus, t * NC + c - 1)
                for kd in range(KD):
                    whi, wlo = w_hi[:, c, kd * P:(kd + 1) * P], w_lo[:, c, kd * P:(kd + 1) * P]
                    eng.matmul(ff1[:, c % 2, :], wlo, hT_hi[:, kd, :], start=(kd == 0), stop=False)
                    eng.matmul(ff1[:, c % 2, :], whi, hT_hi[:, kd, :], start=False, stop=False)
                    ins = eng.matmul(ff1[:, c % 2, :], whi, hT_lo[:, kd, :], start=False, stop=(kd == KD - 1))
                ins.then_inc(ff1_done, 1)

            def output(t, c):
                pe.wait_ge(g_lo_ready, t * NC + c + 1)
                for kd in range(KD):
                    o = D + kd * P
                    whi, wlo = w_hi[:, c, o:o + P], w_lo[:, c, o:o + P]
                    eng.matmul(ff2[:, kd, :], wlo, g_hi[:, c % 2, :], start=(c == 0), stop=False)
                    eng.matmul(ff2[:, kd, :], whi, g_hi[:, c % 2, :], start=False, stop=False)
                    ins = eng.matmul(ff2[:, kd, :], whi, g_lo[:, c % 2, :], start=False, stop=(c == NC - 1))
                ins.then_inc(ff2_done, 1)

            pe.wait_ge(consts, 1)
            for m in range(2 * NT):
                mask_tile(m % NT, m + 1, m < 2)
            sj_turn(0, 1, None)
            r_turn(0, 1, None)
            for q in range(NQ):
                aggregate(0, 0, q, 1, True)
            n1_turn(0)
            r_turn(1, 1, 1)
            for q in range(NQ):
                aggregate(0, 1, q, 1, False)
            pe.wait_ge(w_split, NC)
            pe.wait_ge(src_ready, 2 * NT)

            with pe.Fori(0, PAIRS) as i:
                for k in range(STEPS):
                    t = i * STEPS + k
                    ab, ah, _l = attend_slot(k + 2)
                    n_sj = i * (STEPS // 2) + (k + 2) // 2 + 1
                    if k % 4 == 0:
                        pe.wait_ge(w_split, (i * L + k // 4 + 1) * NC)
                    pe.wait_ge(y2_ready, t + 1)
                    if k > 8 or k == 0:
                        pe.wait_ge(src_ready, masks_before(i, max(k, 8)))
                    for c in range(NC):
                        hidden(t, c)
                        if c == 1 and ah == 0:
                            sj_turn(ab, x_count(i, k + 2), t + 2)
                        if c >= 2:
                            output(t, c - 2)
                        if c == 4:
                            n1_turn(t + 1)
                        if c == 7:
                            r_turn(t + 2, n_sj, t + 2)
                    output(t, NC - 2)
                    output(t, NC - 1)
                    for q in range(NQ):
                        aggregate(ab, t + 2, q, x_count(i, k + 2), False)
                        if q == 1:
                            pe.wait_ge(y2_ready, t + 2)
                            pe.wait_ge(gelus, t * NC + NC)
                            for it in range(HT):
                                for kd in range(KD):
                                    o = (it % 2) * D + kd * P
                                    ins = eng.transpose(ff1[:, it // 2, o:o + P],
                                                        hT[:, k % 2, kd, it * P:(it + 1) * P], ident[:, :])
                            ins.then_inc(y2_turned, 1)
                        if k >= 8:
                            if q == 0:
                                pe.wait_ge(y2_ready, t + 2)
                            mask_tile((k % 2) * 4 + q, masks_before(i, k) + q + 1, False)


_INS = ['x', 'adj', 'L0_gnn_attn_w', 'L0_gnn_attn_b', 'L0_gnn_W1', 'L0_gnn_b1', 'L0_gnn_W2', 'L0_gnn_b2',
        'L0_gnn_g1', 'L0_gnn_beta1', 'L0_gnn_g2', 'L0_gnn_beta2']


def kernel(**inputs):
    import numpy as _np
    import concourse.bacc as _bacc
    from concourse import mybir as _mybir
    from concourse.bass_utils import run_bass_kernel_spmd as _run

    nc = _bacc.Bacc("TRN2", target_bir_lowering=False, num_devices=1)
    arrays, args = {}, []
    for name in _INS:
        a = _np.ascontiguousarray(inputs[name])
        arrays[f"in_{name}_dram"] = a
        args.append(nc.dram_tensor(f"in_{name}_dram", a.shape, _mybir.dt.from_np(a.dtype), kind="ExternalInput").ap())
    out = nc.dram_tensor("out_0_dram", (B, N, D), _mybir.dt.float32, kind="ExternalOutput").ap()
    gnn_kernel(nc, *args, out)
    r = _run(nc, [arrays], core_ids=[0])
    return r.results[0]["out_0_dram"]
```

```python
import concourse.bass as bass
from concourse import mybir
from contextlib import ExitStack

P = 128
B, N, D = 8, 1024, 256
L = 3
FF = 4 * D
NT = N // P
KD = D // P
NC = FF // P
HALF = N // 2
HT = HALF // P
NG = 3
NE = 4
NP = 3
PAIRS = B // 2
STEPS = L * 2 * 2
DX = D + 2
EPS = 1e-5
SLOPE = 0.2


def gnn_kernel(nc, x_d, adj_d, attn_w, attn_b, W1, b1, W2, b2, g1, beta1, g2, beta2, out_d):
    f32, f32r = mybir.dt.float32, mybir.dt.float32r
    bf16, u8, i32 = mybir.dt.bfloat16, mybir.dt.uint8, mybir.dt.int32
    ALU, ACT, AX = mybir.AluOpType, mybir.ActivationFunctionType, mybir.AxisListType

    ctx = ExitStack()
    with ctx:
        def sb(name, shape, dt):
            return ctx.enter_context(nc.sbuf_tensor(name, shape, dt))

        def sem(name):
            return ctx.enter_context(nc.semaphore(name))

        w_hi = sb("w_hi", [P, NC, 2 * D], f32r)
        w_lo = sb("w_lo", [P, NC, 2 * D], f32r)
        w_stage = sb("w_stage", [P, 2, 2 * D], f32)
        x = [sb(f"x{b}", [P, NT, D], f32) for b in range(2)]
        x_hi = [sb(f"x_hi{b}", [P, NT, DX], f32r) for b in range(2)]
        x_lo = [sb(f"x_lo{b}", [P, NT, DX], f32r) for b in range(2)]
        mask_src = [sb(f"mask_src{b}", [P, NT, N], u8) for b in range(2)]
        mask_dst = [sb(f"mask_dst{b}", [P, NT, N], u8) for b in range(2)]
        s = [sb(f"s{b}", [P, NT, 3], f32) for b in range(2)]
        adj_stage = sb("adj_stage", [P, N], i32)
        mask_bf = sb("mask_bf", [P, 2, N], bf16)
        sj_row = sb("sj_row", [P, N], f32)
        r_rows = sb("r_rows", [P, 2, HALF], f32)
        e1 = sb("e1", [P, NE, HALF], f32)
        e2 = sb("e2", [P, 2, HALF], f32)
        p_hi = sb("p_hi", [P, NP, HALF], f32r)
        p_lo = sb("p_lo", [P, NP, HALF], f32r)
        y1 = sb("y1", [P, HT, D], f32)
        hT = sb("hT", [P, 2, KD, HALF], f32)
        hT_hi = sb("hT_hi", [P, KD, HALF], f32r)
        hT_lo = sb("hT_lo", [P, KD, HALF], f32r)
        g = sb("g", [P, 2, HALF], f32)
        g_hi = sb("g_hi", [P, NG, HALF], f32r)
        g_lo = sb("g_lo", [P, NG, HALF], f32r)
        n2 = sb("n2", [P, HT, D], f32)
        x_first = sb("x_first", [P, HT, D], f32)
        w_row = sb("w_row", [P, 2, D], f32)
        g2_row = sb("g2_row", [P, D], f32)
        beta2_row = sb("beta2_row", [P, D], f32)
        b1_col = sb("b1_col", [P, L, NC], f32)
        b2_col = sb("b2_col", [P, L, KD], f32)
        g1_col = sb("g1_col", [P, L, KD], f32)
        beta1_col = sb("beta1_col", [P, L, KD], f32)
        attn_b_col = sb("attn_b_col", [P, L], f32)
        ident = sb("ident", [P, P], f32)
        ident_bf = sb("ident_bf", [P, P], bf16)
        eye = sb("eye", [P, P], i32)
        unused = sb("unused", [P, 2, D], bf16)
        bn1 = sb("bn1", [P, HT, 6], f32)
        mv1 = sb("mv1", [P, HT, 2], f32)
        rstd1 = sb("rstd1", [P, HT], f32)
        bn2 = sb("bn2", [P, HT, 6], f32)
        mv2 = sb("mv2", [P, HT, 2], f32)
        rstd2 = sb("rstd2", [P, HT], f32)
        power = sb("power", [P, HT], f32)
        minus = sb("minus", [P, HT], f32)
        shift1 = sb("shift1", [P, HT], f32)
        shift2 = sb("shift2", [P, HT], f32)
        gate_cell = sb("gate_cell", [P, 1], f32)
        table_cell = sb("table_cell", [P, 2], f32)
        eps = sb("eps", [P, HT], f32)
        r_sum = sb("r_sum", [P, HT], f32)
        sj_min = sb("sj_min", [P, 1], f32)
        sj_max = sb("sj_max", [P, HT], f32)
        z0 = sb("z0", [P, HT], f32)
        zm = sb("zm", [P, HT], f32)
        row_max = sb("row_max", [P, HT], f32)
        r_col = sb("r_col", [P, 2, HT], f32)

        agg = ctx.enter_context(nc.psum_tensor("agg", [P, 4, 512], f32))
        ff1 = ctx.enter_context(nc.psum_tensor("ff1", [P, 2, 512], f32))
        ff2 = ctx.enter_context(nc.psum_tensor("ff2", [P, 2, 512], f32))

        params_in = sem("params_in")
        rows_in = sem("rows_in")
        x_in = sem("x_in")
        x0_in = sem("x0_in")
        adj_in = sem("adj_in")
        w_in = [sem(f"w_in{q}") for q in range(2)]
        out_done = sem("out_done")
        consts = sem("consts")
        diag_added = sem("diag_added")
        mask_ready = sem("mask_ready")
        dst_ready = sem("dst_ready")
        mask_turned = sem("mask_turned")
        src_ready = sem("src_ready")
        w_split_hi = sem("w_split_hi")
        w_split = sem("w_split")
        x_hi_ready = sem("x_hi_ready")
        x_lo_ready = sem("x_lo_ready")
        s_ready = sem("s_ready")
        sj_turned = sem("sj_turned")
        sj_copied = sem("sj_copied")
        cols_ready = sem("cols_ready")
        r_turned = sem("r_turned")
        r_copied = sem("r_copied")
        exps = sem("exps")
        maxed = sem("maxed")
        p_hi_ready = sem("p_hi_ready")
        p_lo_ready = sem("p_lo_ready")
        agg_done = sem("agg_done")
        agg_read = sem("agg_read")
        stats1 = sem("stats1")
        rstd1_ready = sem("rstd1_ready")
        n1_ready = sem("n1_ready")
        n1_turned = sem("n1_turned")
        hT_ready = sem("hT_ready")
        hT_hi_ready = sem("hT_hi_ready")
        hT_lo_ready = sem("hT_lo_ready")
        ff1_done = sem("ff1_done")
        gelus = sem("gelus")
        g_hi_ready = sem("g_hi_ready")
        g_lo_ready = sem("g_lo_ready")
        ff2_done = sem("ff2_done")
        y2_ready = sem("y2_ready")
        y2_turned = sem("y2_turned")
        stats2 = sem("stats2")
        rstd2_ready = sem("rstd2_ready")
        n2_ready = sem("n2_ready")
        x_ready = sem("x_ready")
        x2_ready = sem("x2_ready")
        masked = sem("masked")
        stats3 = sem("stats3")
        rstd3_ready = sem("rstd3_ready")
        out_ready = sem("out_ready")
        dve_link = sem("dve_link")
        pool_link = sem("pool_link")

        class Links:
            def __init__(self, eng, own, per_round):
                self.eng, self.own, self.per_round, self.n, self.round = eng, own, per_round, 0, None

            def after(self, ins):
                self.n += 1
                ins.then_inc(self.own, 1)
                self.eng.wait_ge(self.own, self.n if self.round is None
                                 else self.round * self.per_round + self.n)

        def masks_before(i, k):
            return 16 if i is None else i * 16 + (16 + 4 * (k - 8))

        def x_count(i, kk):
            if i is None:
                return kk // 2 + 1
            return i * 10 + {1: 2, 2: 4, 3: 6, 4: 8, 5: 10, 6: 11}[kk // 2]

        def feed_slot(k):
            return (k // 2) % 2, k % 2, k // 4

        def attend_slot(k):
            return (k // 2) % 2, k % 2, (k // 4) % L

        block = ctx.enter_context(nc.Block())

        @block.sync
        def _(sp):
            def load_rows(score_layer, norm_layer):
                sp.dma_start(w_row[:, :, :], attn_w[score_layer, :].rearrange("(a c) -> a c", a=2)
                             .partition_broadcast(P)).then_inc(rows_in, 16)
                sp.dma_start(g2_row[:, :], g2[norm_layer, :].partition_broadcast(P)).then_inc(rows_in, 16)
                sp.dma_start(beta2_row[:, :], beta2[norm_layer, :].partition_broadcast(P)).then_inc(rows_in, 16)

            def load_chunk(layer, c, n_split):
                if n_split is not None:
                    sp.wait_ge(w_split, n_split)
                sp.dma_start(w_stage[:, c % 2, 0:D].rearrange("p (k n) -> p k n", k=KD),
                             W1[layer, :, c * P:(c + 1) * P].rearrange("(k p) n -> p k n", p=P)).then_inc(w_in[c % 2], 16)
                sp.dma_start(w_stage[:, c % 2, D:2 * D], W2[layer, c * P:(c + 1) * P, :]).then_inc(w_in[c % 2], 16)

            def load_adj(batch, it, first, n_mask):
                if not first:
                    sp.wait_ge(mask_ready, n_mask)
                sp.dma_start(adj_stage[:, :], adj_d[batch, it * P:(it + 1) * P, :]).then_inc(adj_in, 16)

            load_rows(0, 0)
            sp.dma_start(x[0][:, :, :], x_d[0, :, :].rearrange("(t p) d -> p t d", p=P)).then_inc(x_in, 16)
            load_adj(0, 0, True, 0)
            for dst, src in ((b1_col, b1), (b2_col, b2), (g1_col, g1), (beta1_col, beta1)):
                sp.dma_start(dst[:, :, :], src.rearrange("l (c p) -> p l c", p=P),
                             allow_slow_non_contiguous=True).then_inc(params_in, 16)
            sp.dma_start(attn_b_col[:, :], attn_b.partition_broadcast(P)).then_inc(params_in, 16)
            for m in range(1, 2 * NT):
                load_adj(m // NT, m % NT, False, m)
                if m == 1:
                    sp.wait_ge(x_in, 16)
                    sp.dma_start(x[1][:, :, :], x_d[1, :, :].rearrange("(t p) d -> p t d", p=P)).then_inc(x_in, 16)
                if m % 2 == 0:
                    c = m // 2 - 1
                    load_chunk(0, c, c - 1 if c >= 2 else None)
            load_chunk(0, NC - 1, NC - 2)
            sp.wait_ge(s_ready, 2)
            load_rows(1, 0)

            def store(i, k):
                sp.wait_ge(out_ready, i * 4 + k - 7)
                sp.dma_start(out_d[i * 2 + (k - 8) // 2, (k % 2) * HALF:(k % 2 + 1) * HALF, :]
                             .rearrange("(t p) d -> p t d", p=P), n2[:, :, :]).then_inc(out_done, 16)

            with sp.Fori(0, PAIRS) as i:
                nxt = (i + 1) % PAIRS
                for k in range(STEPS):
                    t = i * STEPS + k
                    b, h, layer = feed_slot(k)

                    def adj_tile(q):
                        load_adj(nxt * 2 + (k - 8) // 2, (k % 2) * 4 + q, False, masks_before(i, k) + q)

                    def next_chunk(c):
                        load_chunk((layer + 1) % L, c, i * (L * NC) + (layer + 1) * NC + c - 1)

                    if k >= 8:
                        adj_tile(0)
                    if k in (4, 8):
                        sp.wait_ge(s_ready, i * 10 + k + 2)
                        load_rows({4: 2, 8: 0}[k], layer)
                    if k > 8:
                        store(i, k - 1)
                    if k >= 8:
                        sp.dma_start(x_first[:, :, :], x_d[i * 2 + b, h * HALF:(h + 1) * HALF, :]
                                     .rearrange("(t p) d -> p t d", p=P)).then_inc(x0_in, 16)
                        adj_tile(1)
                    if k in (8, 10):
                        sp.wait_ge(agg_read, t + 2)
                        sp.dma_start(x[b][:, :, :], x_d[nxt * 2 + b, :, :]
                                     .rearrange("(t p) d -> p t d", p=P)).then_inc(x_in, 16)
                    if k % 4 == 3:
                        for c in range(4):
                            next_chunk(c)
                    if k >= 8:
                        adj_tile(2)
                    if k % 4 == 3:
                        for c in range(4, NC):
                            next_chunk(c)
                    if k >= 8:
                        adj_tile(3)
                    if k == 11:
                        store(i, k)
                        sp.wait_ge(s_ready, i * 10 + 12)
                        load_rows(1, 0)
            sp.wait_ge(out_done, 16 * B * 2)
            sp.wait_ge(rows_in, 48 * (2 + 3 * PAIRS))

        @block.gpsimd
        def _(pool):
            links = Links(pool, pool_link, (2 * 2 + 1) * STEPS + 4 * 2)
            eng = nc.gpsimd

            def split_lo(dst, value, hi, ready):
                eng.tensor_tensor(dst, value, hi.bitcast(f32), ALU.subtract).then_inc(ready, 1)

            def mask_tile(it, n_in):
                pool.wait_ge(adj_in, n_in * 16)
                d = adj_stage[:, it * P:(it + 1) * P]
                eng.tensor_tensor(d, d, eye[:, :], ALU.add).then_inc(diag_added, 1)

            def inv_std(mv, dst, shift, stats, n_stats, ready):
                pool.wait_ge(stats, n_stats)
                links.after(eng.tensor_tensor(dst[:, :], mv[:, :, 1], eps[:, :], ALU.add))
                eng.tensor_tensor(shift[:, :], mv[:, :, 0], minus[:, :], ALU.mult)
                links.after(eng.tensor_tensor(dst[:, :], dst[:, :], power[:, :], ALU.pow))
                eng.tensor_tensor(shift[:, :], shift[:, :], dst[:, :], ALU.mult).then_inc(ready, 1)

            def new_batch_lo(b, n):
                pool.wait_ge(x_hi_ready, n)
                split_lo(x_lo[b][:, :, 0:D], x[b][:, :, :], x_hi[b][:, :, 0:D], x_lo_ready)

            def late_part(i, k):
                b, h, layer = feed_slot(k)
                rows = slice(h * HT, (h + 1) * HT)
                if layer < L - 1:
                    pool.wait_ge(x_hi_ready, i * 10 + k + 3)
                    split_lo(x_lo[b][:, rows, 0:D], x[b][:, rows, :], x_hi[b][:, rows, 0:D], x_lo_ready)
                else:
                    inv_std(mv2, rstd2, shift2, stats3, i * 4 + k - 7, rstd3_ready)

            def chunk_lo(c, n):
                pool.wait_ge(w_split_hi, n)
                split_lo(w_lo[:, c, :], w_stage[:, c % 2], w_hi[:, c, :], w_split)

            def prob_lo(a, j):
                pool.wait_ge(p_hi_ready, a * NT + j + 1)
                split_lo(p_lo[:, j % NP], e1[:, j % NE], p_hi[:, j % NP], p_lo_ready)

            eng.memset(ident[:, :], 0.0).then_inc(pool_link, 1)
            eng.memset(eye[:, :], 0).then_inc(pool_link, 1)
            eng.memset(power[:, :], -0.5)
            eng.memset(eps[:, :], EPS)
            eng.memset(minus[:, :], -1.0)
            for b in range(2):
                eng.memset(x_hi[b][:, :, D:D + 1].bitcast(f32), 1.0)
                eng.memset(x_hi[b][:, :, D + 1:DX].bitcast(f32), 0.0)
                eng.memset(x_lo[b][:, :, D:DX].bitcast(f32), 0.0)
            pool.wait_ge(pool_link, 2)
            eng.affine_select(out=ident[:, :], in_=ident[:, :], compare_op=ALU.not_equal, fill=1.0, base=0,
                              pattern=[[-1, P]], channel_multiplier=1).then_inc(pool_link, 1)
            pool.wait_ge(pool_link, 3)
            eng.tensor_copy(eye[:, :], ident[:, :]).then_inc(pool_link, 1)
            eng.tensor_copy(ident_bf[:, :], ident[:, :]).then_inc(consts, 1)
            pool.wait_ge(pool_link, 4)
            links.n = 4
            for m in range(2 * NT):
                mask_tile(m % NT, m + 1)
                if m == 0:
                    new_batch_lo(0, 1)
                if m == 2:
                    new_batch_lo(1, 2)
                if m >= 2 and m % 2 == 0:
                    chunk_lo(m // 2 - 1, m // 2)
            chunk_lo(NC - 1, NC)
            for j in range(NT):
                prob_lo(0, j)
            inv_std(mv1, rstd1, shift1, stats1, 1, rstd1_ready)
            pool.wait_ge(hT_hi_ready, 1)
            split_lo(hT_lo[:, :, :], hT[:, 0], hT_hi[:, :, :], hT_lo_ready)
            for j in range(NT):
                prob_lo(1, j)
            n_ahead = links.n

            with pool.Fori(0, PAIRS) as i:
                links.round, links.n = i, n_ahead
                for k in range(STEPS):
                    t = i * STEPS + k
                    b, h, layer = feed_slot(k)
                    n_chunk = i * (L * NC) + (layer + 1) * NC
                    inv_std(mv1, rstd1, shift1, stats1, t + 2, rstd1_ready)
                    for c in range(NC):
                        pool.wait_ge(g_hi_ready, t * NC + c + 1)
                        split_lo(g_lo[:, c % NG], g[:, c % 2], g_hi[:, c % NG], g_lo_ready)
                        if c == 2 and k > 0:
                            late_part(i, k - 1)
                        if k >= 8 and c in (1, 5):
                            mask_tile((k % 2) * 4 + c // 4, masks_before(i, k) + c // 4 + 1)
                        if k in (9, 11) and c == 6:
                            new_batch_lo((k - 8) // 2, i * 10 + {9: 11, 11: 12}[k])
                        if k % 4 == 3 and c >= 4:
                            chunk_lo(c - 4, n_chunk + c - 3)
                    pool.wait_ge(hT_hi_ready, t + 2)
                    split_lo(hT_lo[:, :, :], hT[:, (k + 1) % 2], hT_hi[:, :, :], hT_lo_ready)
                    for j in range(NT):
                        if k >= 8 and j in (3, 5):
                            q = (j + 1) // 2
                            mask_tile((k % 2) * 4 + q, masks_before(i, k) + q + 1)
                        prob_lo(t + 2, j)
                        if k % 4 == 3 and 1 <= j <= 4:
                            chunk_lo(j + 3, n_chunk + j + 4)
                        if j == 5:
                            inv_std(mv2, rstd2, shift2, stats2, t + 1, rstd2_ready)
                    pool.wait_ge(n2_ready, t + 2)
                    if k % 4 == 0:
                        pool.wait_ge(rows_in, (i * 3 + 2 + layer) * 48)
                    first = slice(0, HT // 2)
                    g2_t, beta2_t = (r[:, :].unsqueeze(1).broadcast_to([P, HT // 2, D]) for r in (g2_row, beta2_row))
                    links.after(eng.tensor_tensor(n2[:, first, :], n2[:, first, :], g2_t, ALU.mult))
                    dst = x[b][:, h * HT:h * HT + HT // 2, :] if layer < L - 1 else n2[:, first, :]
                    eng.tensor_tensor(dst, n2[:, first, :], beta2_t, ALU.add).then_inc(x_ready, 1)
                    if k == 11:
                        late_part(i, k)
                assert links.n - n_ahead == links.per_round

        @block.scalar
        def _(act):
            eng = nc.scalar

            def mask_dst_tile(b, it, n):
                act.wait_ge(mask_ready, n)
                eng.activation(mask_dst[b][:, it, :], mask_bf[:, it % 2, :], ACT.Copy).then_inc(dst_ready, 1)

            def mask_src_tile(b, it, n):
                act.wait_ge(mask_turned, n)
                eng.activation(mask_src[b][:, :, it * P:(it + 1) * P],
                               ff2[:, it % 2, :].bitcast(bf16).rearrange("p (j i) -> p j i", j=NT),
                               ACT.Copy).then_inc(src_ready, 1)

            def sj_copy(n):
                act.wait_ge(sj_turned, n)
                eng.activation(sj_row[:, :].rearrange("p (a n) -> p a n", a=2), agg[:, 2:4, :],
                               ACT.Copy).then_inc(sj_copied, 1)

            def r_copy(a):
                act.wait_ge(r_turned, a + 1)
                eng.activation(r_rows[:, :, :], agg[:, 2:4, :], ACT.Copy).then_inc(r_copied, 1)

            def hT_copy(a, buf, layer):
                act.wait_ge(n1_turned, a + 1)
                for kd in range(KD):
                    ins = eng.activation(hT[:, buf, kd, :], agg[:, kd, :], ACT.Identity,
                                         bias=beta1_col[:, layer, kd:kd + 1], scale=g1_col[:, layer, kd:kd + 1])
                ins.then_inc(hT_ready, 1)

            def normalize(dst, src, rstd, shift, ready, n, done):
                act.wait_ge(ready, n)
                for it in range(HT):
                    ins = eng.activation(dst[:, it, :], src(it), ACT.Identity,
                                         bias=shift[:, it:it + 1], scale=rstd[:, it:it + 1])
                ins.then_inc(done, 1)

            def exp_tile(b, a, j, e1_free, e2_free):
                if e1_free:
                    act.wait_ge(p_lo_ready, a * NT + j - NE + 1)
                if e2_free:
                    act.wait_ge(maxed, a * NT + j - 1)
                if j == 0:
                    act.wait_ge(r_copied, a + 1)
                eng.activation(e1[:, j % NE, :], r_rows[:, 0, :], ACT.Exp, bias=s[b][:, j, 1:2], scale=1.0)
                eng.activation(e2[:, j % 2, :], r_rows[:, 1, :], ACT.Exp, bias=s[b][:, j, 2:3],
                               scale=1.0).then_inc(exps, 1)

            def late_part(i, k):
                b, h, layer = feed_slot(k)
                rows = slice(h * HT, (h + 1) * HT)
                if layer < L - 1:
                    act.wait_ge(x_ready, i * STEPS + k + 1)
                    act.wait_ge(x2_ready, i * STEPS + k + 1)
                    eng.activation(x_hi[b][:, rows, 0:D], x[b][:, rows, :], ACT.Copy).then_inc(x_hi_ready, 1)
                else:
                    normalize(n2, lambda it: n2[:, it, :], rstd2, shift2, rstd3_ready, i * 4 + k - 7, out_ready)

            act.wait_ge(x_in, 16)
            eng.activation(x_hi[0][:, :, 0:D], x[0][:, :, :], ACT.Copy).then_inc(x_hi_ready, 1)
            for m in range(2 * NT):
                mask_dst_tile(m // NT, m % NT, m + 1)
                mask_src_tile(m // NT, m % NT, m + 1)
                if m == 1:
                    act.wait_ge(x_in, 32)
                    eng.activation(x_hi[1][:, :, 0:D], x[1][:, :, :], ACT.Copy).then_inc(x_hi_ready, 1)
            act.wait_ge(params_in, 16 * 5)
            sj_copy(1)
            r_copy(0)
            for j in range(NT):
                exp_tile(0, 0, j, j >= NE, j >= 2)
            normalize(y1, lambda it: y1[:, it, :], rstd1, shift1, rstd1_ready, 1, n1_ready)
            hT_copy(0, 0, 0)
            r_copy(1)
            for j in range(NT):
                exp_tile(0, 1, j, True, True)

            with act.Fori(0, PAIRS) as i:
                for k in range(STEPS):
                    t = i * STEPS + k
                    b, h, layer = feed_slot(k)
                    ab, ah, _l = attend_slot(k + 2)
                    mb, mt = (k - 8) // 2, (k % 2) * 4
                    for c in range(NC):
                        act.wait_ge(ff1_done, t * NC + c + 1)
                        if c >= 2:
                            act.wait_ge(g_lo_ready, t * NC + c - 1)
                        eng.activation(g[:, c % 2, :], ff1[:, c % 2, :], ACT.Gelu,
                                       bias=b1_col[:, layer, c:c + 1], scale=1.0).then_inc(gelus, 1)
                        if c == 0:
                            normalize(y1, lambda it: y1[:, it, :], rstd1, shift1, rstd1_ready, t + 2, n1_ready)
                        if k > 0 and c == (1 if k <= 8 else 4):
                            late_part(i, k - 1)
                        if k in (9, 11) and c == 2:
                            nb = (k - 8) // 2
                            act.wait_ge(x_in, (i * 2 + nb + 3) * 16)
                            eng.activation(x_hi[nb][:, :, 0:D], x[nb][:, :, :], ACT.Copy).then_inc(x_hi_ready, 1)
                        if c == 4 and ah == 0:
                            sj_copy(i * (STEPS // 2) + (k + 2) // 2 + 1)
                        if c == 5:
                            hT_copy(t + 1, (k + 1) % 2, ((k + 1) // 4) % L)
                        if k >= 8 and c in (5, 7):
                            mask_dst_tile(mb, mt + (c - 5) // 2, masks_before(i, k) + (c - 5) // 2 + 1)
                    eng.activation(table_cell[:, 0:1], ident[:, 0:1], ACT.Exp)
                    r_copy(t + 2)
                    for j in range(NT):
                        exp_tile(ab, t + 2, j, True, True)
                        if k >= 8 and j in (4, 5, 7):
                            q = {4: 0, 5: 1, 7: 2}[j]
                            mask_src_tile(mb, mt + q, masks_before(i, k) + q + 1)
                        if k >= 8 and j == 6:
                            mask_dst_tile(mb, mt + 2, masks_before(i, k) + 3)
                    eng.activation(table_cell[:, 1:2], ident[:, 0:1], ACT.Gelu)
                    if k > 8:
                        act.wait_ge(out_done, (i * 4 + k - 8) * 16)
                    normalize(n2, lambda it: ff1[:, it // 2, (it % 2) * D:(it % 2 + 1) * D], rstd2, shift2,
                              rstd2_ready, t + 1, n2_ready)
                    if k >= 8:
                        mask_dst_tile(mb, mt + 3, masks_before(i, k) + 4)
                        mask_src_tile(mb, mt + 3, masks_before(i, k) + 4)
                    if k == 11:
                        late_part(i, k)
                        act.wait_ge(out_done, (i * 4 + 4) * 16)

        @block.vector
        def _(dve):
            eng = nc.vector
            links = Links(dve, dve_link, STEPS * (3 + HT // 2 + 3 + 1) + STEPS // 2 * 2 + (L - 1) * 4 * HT
                          + 4 * 2 + 2 * NT)

            def gate():
                eng.memset(gate_cell[:, :], 0.0)

            def mask_tile(q, n, first):
                dve.wait_ge(diag_added, n)
                if not first:
                    dve.wait_ge(dst_ready, n - 2)
                    dve.wait_ge(mask_turned, n - 2)
                eng.tensor_scalar(mask_bf[:, q, :], adj_stage[:, :], 0.0, None, ALU.is_gt).then_inc(mask_ready, 1)

            def scores(b, tiles):
                for it in tiles:
                    for side in range(2):
                        ins = eng.tensor_tensor_reduce(
                            out=unused[:, side, :], in0=x[b][:, it, :], in1=w_row[:, side, :], scale=1.0,
                            scalar=0.0, op0=ALU.mult, op1=ALU.add, accum_out=s[b][:, it, side:side + 1])
                    links.after(ins)
                sl = slice(tiles[0], tiles[-1] + 1)
                eng.tensor_scalar(s[b][:, sl, 2], s[b][:, sl, 1], SLOPE, None, ALU.mult).then_inc(s_ready, 1)

            def chunk_hi(c, n):
                dve.wait_ge(w_in[c % 2], n * 32)
                eng.tensor_copy(w_hi[:, c, :], w_stage[:, c % 2]).then_inc(w_split_hi, 1)

            def source_min(n):
                dve.wait_ge(sj_copied, n)
                links.after(eng.tensor_reduce(out=sj_min[:, :], in_=sj_row[:, :], axis=AX.X, op=ALU.min))
                links.after(eng.tensor_scalar(sj_row[:, :], sj_row[:, :], sj_min[:, :], None, ALU.subtract))

            def row_maxima(b, its):
                for it in its:
                    ins = eng.tensor_tensor_reduce(
                        out=e2[:, it % 2, :].bitcast(bf16), in0=sj_row[:, :], in1=mask_dst[b][:, it, :], scale=1.0, scalar=0.0,
                        op0=ALU.mult, op1=ALU.max, accum_out=sj_max[:, it % HT:it % HT + 1])
                    if it % 2 == 1:
                        links.after(ins)
                        gate()

            def shift_columns(b, h, layer):
                si = s[b][:, h * HT:(h + 1) * HT, 0]
                links.after(eng.tensor_scalar(z0[:, :], si, attn_b_col[:, layer:layer + 1], None, ALU.add))
                links.after(eng.scalar_tensor_tensor(out=zm[:, :], in0=sj_max[:, :], scalar=sj_min[:, :],
                                                     in1=z0[:, :], op0=ALU.add, op1=ALU.add))
                links.after(eng.scalar_tensor_tensor(out=row_max[:, :], in0=zm[:, :], scalar=SLOPE,
                                                     in1=zm[:, :], op0=ALU.mult, op1=ALU.max))
                eng.tensor_tensor(r_col[:, 0, :], z0[:, :], row_max[:, :], ALU.subtract)
                eng.scalar_tensor_tensor(out=r_col[:, 1, :], in0=z0[:, :], scalar=SLOPE, in1=row_max[:, :],
                                         op0=ALU.mult, op1=ALU.subtract).then_inc(cols_ready, 1)

            def probs(b, h, a, tiles, p_free):
                def hi(j):
                    dve.wait_ge(masked, a * NT + j + 1)
                    if p_free or j >= NP:
                        dve.wait_ge(agg_done, a * NT + j - NP + 1)
                    eng.tensor_copy(p_hi[:, j % NP, :], e1[:, j % NE, :]).then_inc(p_hi_ready, 1)

                for j in tiles:
                    e = e1[:, j % NE, :]
                    dve.wait_ge(exps, a * NT + j + 1)
                    eng.tensor_tensor(e, e, e2[:, j % 2, :], ALU.max).then_inc(maxed, 1)
                    if j > 1:
                        hi(j - 1)
                    dve.wait_ge(maxed, a * NT + j + 1)
                    eng.tensor_tensor(e, e, mask_src[b][:, j, h * HALF:(h + 1) * HALF], ALU.min).then_inc(masked, 1)
                    if j == 0:
                        hi(0)
                if tiles[-1] == NT - 1:
                    hi(NT - 1)

            def residual1(b, h, a):
                dve.wait_ge(agg_done, a * NT + NT)
                for it in range(HT):
                    ins = eng.reciprocal(r_sum[:, it:it + 1], agg[:, it, D:D + 1])
                links.after(ins)
                for it in range(HT):
                    ins = eng.scalar_tensor_tensor(out=y1[:, it, :], in0=agg[:, it, 0:D], scalar=r_sum[:, it:it + 1],
                                                   in1=x[b][:, h * HT + it, :], op0=ALU.mult, op1=ALU.add)
                ins.then_inc(agg_read, 1)
                dve.wait_ge(agg_read, a + 1)

            def mean_var(src, bn, mv, ready):
                for it in range(HT):
                    ins = eng.bn_stats(bn[:, it, :], src(it))
                links.after(ins)
                gate()
                for it in range(HT):
                    ins = eng.bn_aggr(mv[:, it, :], bn[:, it, :])
                ins.then_inc(ready, 1)

            def hT_split(a, buf):
                dve.wait_ge(hT_ready, a + 1)
                eng.tensor_copy(hT_hi[:, :, :], hT[:, buf]).then_inc(hT_hi_ready, 1)

            def late_scaling(i, k):
                b, h, layer = feed_slot(k)
                dve.wait_ge(n2_ready, i * STEPS + k + 2)
                if k % 4 == 0:
                    dve.wait_ge(rows_in, (i * 3 + 2 + layer) * 48)
                last = slice(HT // 2, HT)
                g2_t, beta2_t = (r[:, :].unsqueeze(1).broadcast_to([P, HT // 2, D]) for r in (g2_row, beta2_row))
                links.after(eng.tensor_tensor(n2[:, last, :], n2[:, last, :], g2_t, ALU.mult))
                dst = x[b][:, h * HT + HT // 2:(h + 1) * HT, :] if layer < L - 1 else n2[:, last, :]
                eng.tensor_tensor(dst, n2[:, last, :], beta2_t, ALU.add).then_inc(x2_ready, 1)

            def late_rest(i, k):
                b, h, layer = feed_slot(k)
                dve.wait_ge(x2_ready, i * STEPS + k + 1)
                dve.wait_ge(x_ready, i * STEPS + k + 1)
                if layer < L - 1:
                    scores(b, range(h * HT, (h + 1) * HT))
                else:
                    dve.wait_ge(x0_in, (i * 4 + k - 7) * 16)
                    links.after(eng.tensor_tensor(n2[:, :, :], n2[:, :, :], x_first[:, :, :], ALU.add))
                    mean_var(lambda it: n2[:, it, :], bn2, mv2, stats3)

            eng.memset(bn1[:, 0, :], 0.0).then_inc(y2_ready, 1)
            eng.memset(bn2[:, 0, :], 0.0).then_inc(n2_ready, 1)
            dve.wait_ge(rows_in, 48)
            for m in range(2 * NT):
                mask_tile(m % 2, m + 1, m < 2)
                if m == 0:
                    dve.wait_ge(x_in, 16)
                    scores(0, range(NT))
                if m == 2:
                    dve.wait_ge(x_in, 32)
                    scores(1, range(NT))
                if m >= 2 and m % 2 == 0:
                    chunk_hi(m // 2 - 1, (m // 2 + 1) // 2)
            chunk_hi(NC - 1, NC // 2)
            dve.wait_ge(params_in, 16 * 5)
            dve.wait_ge(dst_ready, 2 * NT)
            dve.wait_ge(src_ready, 2 * NT)
            source_min(1)
            row_maxima(0, range(HT))
            shift_columns(0, 0, 0)
            probs(0, 0, 0, range(NT), False)
            residual1(0, 0, 0)
            mean_var(lambda it: y1[:, it, :], bn1, mv1, stats1)
            hT_split(0, 0)
            row_maxima(0, range(HT, 2 * HT))
            shift_columns(0, 1, 0)
            probs(0, 1, 1, range(NT), True)
            dve.wait_ge(n1_turned, 1)
            residual1(0, 1, 1)
            mean_var(lambda it: y1[:, it, :], bn1, mv1, stats1)
            n_ahead = links.n

            with dve.Fori(0, PAIRS) as i:
                links.round, links.n = i, n_ahead
                for k in range(STEPS):
                    t = i * STEPS + k
                    b, h, layer = feed_slot(k)
                    ab, ah, al = attend_slot(k + 2)

                    def gelu_hi(c):
                        dve.wait_ge(gelus, t * NC + c + 1)
                        if c >= NG:
                            dve.wait_ge(ff2_done, t * NC + c - NG + 1)
                        eng.tensor_copy(g_hi[:, c % NG], g[:, c % 2]).then_inc(g_hi_ready, 1)

                    def next_hi(c):
                        dve.wait_ge(ff2_done, t * NC + c + 1)
                        chunk_hi(c, i * (L * NC // 2) + ((layer + 1) * NC + c) // 2 + 1)

                    def masks(q):
                        mask_tile(q % 2, masks_before(i, k) + q + 1, False)

                    gelu_hi(0)
                    if k > 0:
                        late_scaling(i, k - 1)
                    gelu_hi(1)
                    if k > 0:
                        late_rest(i, k - 1)
                    gelu_hi(2)
                    if k >= 8:
                        masks(0)
                    gelu_hi(3)
                    if k in (9, 11):
                        nb = (k - 8) // 2
                        dve.wait_ge(x_in, (i * 2 + nb + 3) * 16)
                        dve.wait_ge(rows_in, (i * 3 + 4) * 48)
                        scores(nb, range(NT))
                    if ah == 0:
                        if k + 2 == STEPS:
                            dve.wait_ge(dst_ready, masks_before(i, 10))
                        if k + 2 == 2:
                            dve.wait_ge(dst_ready, masks_before(i, 8))
                        source_min(i * (STEPS // 2) + (k + 2) // 2 + 1)
                    gelu_hi(4)
                    row_maxima(ab, range(ah * HT, ah * HT + 2))
                    if k % 4 == 3:
                        next_hi(0)
                    gelu_hi(5)
                    row_maxima(ab, range(ah * HT + 2, ah * HT + 4))
                    shift_columns(ab, ah, al)
                    if k % 4 == 3:
                        next_hi(1)
                    gelu_hi(6)
                    if k >= 8:
                        masks(1)
                    if k % 4 == 3:
                        next_hi(2)
                    gelu_hi(7)
                    dve.wait_ge(ff1_done, t * NC + NC)
                    hT_split(t + 1, (k + 1) % 2)
                    if k % 4 == 3:
                        next_hi(3)

                    for j in range(NT):
                        probs(ab, ah, t + 2, [j], True)
                        if j == 1:
                            dve.wait_ge(ff2_done, t * NC + NC)
                            for kd in range(KD):
                                ins = eng.scalar_tensor_tensor(
                                    out=hT[:, k % 2, kd, :], in0=ff2[:, kd, :], scalar=b2_col[:, layer, kd:kd + 1],
                                    in1=hT[:, k % 2, kd, :], op0=ALU.add, op1=ALU.add)
                            ins.then_inc(y2_ready, 1)
                        if k % 4 == 3 and 1 <= j <= 4:
                            next_hi(j + 3)
                        if k >= 8 and j in (4, 6):
                            masks(j // 2)
                        if j == 4:
                            dve.wait_ge(y2_turned, t + 1)
                            mean_var(lambda it: ff1[:, it // 2, (it % 2) * D:(it % 2 + 1) * D], bn2, mv2, stats2)
                    residual1(ab, ah, t + 2)
                    mean_var(lambda it: y1[:, it, :], bn1, mv1, stats1)
                    if k == 11:
                        late_scaling(i, k)
                        late_rest(i, k)
                assert links.n - n_ahead == links.per_round

        @block.tensor
        def _(pe):
            eng = nc.tensor

            def mask_tile(it, n, first):
                pe.wait_ge(mask_ready, n)
                if not first:
                    pe.wait_ge(src_ready, n - 2)
                bank = ff2[:, it % 2, :].bitcast(bf16)
                for j in range(NT):
                    ins = eng.transpose(bank[:, j * P:(j + 1) * P], mask_bf[:, it % 2, j * P:(j + 1) * P], ident_bf[:, :])
                ins.then_inc(mask_turned, 1)

            def sj_turn(b, n_s, n_agg):
                pe.wait_ge(s_ready, n_s)
                if n_agg is not None:
                    pe.wait_ge(agg_read, n_agg)
                for j in range(NT):
                    ins = eng.transpose(agg[:, 2 + j // 4, (j % 4) * P:(j % 4 + 1) * P],
                                        s[b][:, j, 1:2].to_broadcast([P, P]), ident[:, :])
                ins.then_inc(sj_turned, 1)

            def r_turn(a, n_sj, n_agg):
                pe.wait_ge(cols_ready, a + 1)
                pe.wait_ge(sj_copied, n_sj)
                if n_agg is not None:
                    pe.wait_ge(agg_read, n_agg)
                for r in range(2):
                    for it in range(HT):
                        ins = eng.transpose(agg[:, 2 + r, it * P:(it + 1) * P],
                                            r_col[:, r, it:it + 1].to_broadcast([P, P]), ident[:, :])
                ins.then_inc(r_turned, 1)

            def aggregate(b, a, jt, n_x, first_step):
                if jt == 0:
                    pe.wait_ge(r_copied, a + 1)
                    pe.wait_ge(x_lo_ready, n_x)
                    if not first_step:
                        pe.wait_ge(hT_ready, a)
                pe.wait_ge(p_lo_ready, a * NT + jt + 1)
                for it in range(HT):
                    hi = p_hi[:, jt % NP, it * P:(it + 1) * P]
                    lo = p_lo[:, jt % NP, it * P:(it + 1) * P]
                    bank = agg[:, it, 0:DX]
                    eng.matmul(bank, hi, x_lo[b][:, jt, :], start=(jt == 0), stop=False)
                    eng.matmul(bank, hi, x_hi[b][:, jt, :], start=False, stop=False)
                    ins = eng.matmul(bank, lo, x_hi[b][:, jt, :], start=False, stop=(jt == NT - 1))
                ins.then_inc(agg_done, 1)

            def n1_turn(a):
                pe.wait_ge(n1_ready, a + 1)
                for kd in range(KD):
                    for it in range(HT):
                        ins = eng.transpose(agg[:, kd, it * P:(it + 1) * P], y1[:, it, kd * P:(kd + 1) * P], ident[:, :])
                ins.then_inc(n1_turned, 1)

            def hidden(t, c):
                if c == 0:
                    pe.wait_ge(n2_ready, t + 1)
                    pe.wait_ge(hT_lo_ready, t + 1)
                if c >= 2:
                    pe.wait_ge(gelus, t * NC + c - 1)
                for kd in range(KD):
                    whi, wlo = w_hi[:, c, kd * P:(kd + 1) * P], w_lo[:, c, kd * P:(kd + 1) * P]
                    eng.matmul(ff1[:, c % 2, :], wlo, hT_hi[:, kd, :], start=(kd == 0), stop=False)
                    eng.matmul(ff1[:, c % 2, :], whi, hT_hi[:, kd, :], start=False, stop=False)
                    ins = eng.matmul(ff1[:, c % 2, :], whi, hT_lo[:, kd, :], start=False, stop=(kd == KD - 1))
                ins.then_inc(ff1_done, 1)

            def output(t, c):
                pe.wait_ge(g_lo_ready, t * NC + c + 1)
                for kd in range(KD):
                    o = D + kd * P
                    whi, wlo = w_hi[:, c, o:o + P], w_lo[:, c, o:o + P]
                    eng.matmul(ff2[:, kd, :], wlo, g_hi[:, c % NG, :], start=(c == 0), stop=False)
                    eng.matmul(ff2[:, kd, :], whi, g_hi[:, c % NG, :], start=False, stop=False)
                    ins = eng.matmul(ff2[:, kd, :], whi, g_lo[:, c % NG, :], start=False, stop=(c == NC - 1))
                ins.then_inc(ff2_done, 1)

            pe.wait_ge(consts, 1)
            for m in range(2 * NT):
                mask_tile(m % NT, m + 1, m < 2)
            sj_turn(0, 1, None)
            r_turn(0, 1, None)
            for j in range(NT):
                aggregate(0, 0, j, 1, True)
            n1_turn(0)
            r_turn(1, 1, 1)
            for j in range(NT):
                aggregate(0, 1, j, 1, False)
            pe.wait_ge(w_split, NC)
            pe.wait_ge(src_ready, 2 * NT)

            with pe.Fori(0, PAIRS) as i:
                for k in range(STEPS):
                    t = i * STEPS + k
                    ab, ah, _l = attend_slot(k + 2)
                    n_sj = i * (STEPS // 2) + (k + 2) // 2 + 1
                    if k % 4 == 0:
                        pe.wait_ge(w_split, (i * L + k // 4 + 1) * NC)
                    for c in range(NC):
                        hidden(t, c)
                        if c == 1:
                            pe.wait_ge(y2_ready, t + 1)
                            if k > 8 or k == 0:
                                pe.wait_ge(src_ready, masks_before(i, max(k, 8)))
                        if 2 <= c < NC - 1:
                            output(t, c - 2)
                        if c == 4 and ah == 0:
                            sj_turn(ab, x_count(i, k + 2), t + 2)
                        if c == 5:
                            n1_turn(t + 1)
                        if c == 7 - ah:
                            r_turn(t + 2, n_sj, t + 2)
                    for c in range(NC - 3, NC):
                        output(t, c)
                    for j in range(NT):
                        aggregate(ab, t + 2, j, x_count(i, k + 2), False)
                        if j == 1:
                            pe.wait_ge(y2_ready, t + 2)
                        if j == 2:
                            pe.wait_ge(gelus, t * NC + NC)
                            for it in range(HT):
                                for kd in range(KD):
                                    o = (it % 2) * D + kd * P
                                    ins = eng.transpose(ff1[:, it // 2, o:o + P],
                                                        hT[:, k % 2, kd, it * P:(it + 1) * P], ident[:, :])
                            ins.then_inc(y2_turned, 1)
                        if k >= 8 and j in (1, 2, 5, 7):
                            q = (1, 2, 5, 7).index(j)
                            mask_tile((k % 2) * 4 + q, masks_before(i, k) + q + 1, False)


_INS = ['x', 'adj', 'L0_gnn_attn_w', 'L0_gnn_attn_b', 'L0_gnn_W1', 'L0_gnn_b1', 'L0_gnn_W2', 'L0_gnn_b2',
        'L0_gnn_g1', 'L0_gnn_beta1', 'L0_gnn_g2', 'L0_gnn_beta2']


def kernel(**inputs):
    import numpy as _np
    import concourse.bacc as _bacc
    from concourse import mybir as _mybir
    from concourse.bass_utils import run_bass_kernel_spmd as _run

    nc = _bacc.Bacc("TRN2", target_bir_lowering=False, num_devices=1)
    arrays, args = {}, []
    for name in _INS:
        a = _np.ascontiguousarray(inputs[name])
        arrays[f"in_{name}_dram"] = a
        args.append(nc.dram_tensor(f"in_{name}_dram", a.shape, _mybir.dt.from_np(a.dtype), kind="ExternalInput").ap())
    out = nc.dram_tensor("out_0_dram", (B, N, D), _mybir.dt.float32, kind="ExternalOutput").ap()
    gnn_kernel(nc, *args, out)
    r = _run(nc, [arrays], core_ids=[0])
    return r.results[0]["out_0_dram"]
```

```python
import concourse.bass as bass
from concourse import mybir
from contextlib import ExitStack

P = 128
B, N, D = 8, 1024, 256
L = 3
FF = 4 * D
NT = N // P
KD = D // P
NC = FF // P
HALF = N // 2
HT = HALF // P
NE = 4
NR = 6
PAIRS = B // 2
STEPS = L * 2 * 2
BR = 32
DX = D + 2
EPS = 1e-5
SLOPE = 0.2


def gnn_kernel(nc, x_d, adj_d, attn_w, attn_b, W1, b1, W2, b2, g1, beta1, g2, beta2, out_d):
    f32, f32r = mybir.dt.float32, mybir.dt.float32r
    bf16, u8, i32 = mybir.dt.bfloat16, mybir.dt.uint8, mybir.dt.int32
    ALU, ACT, AX = mybir.AluOpType, mybir.ActivationFunctionType, mybir.AxisListType

    ctx = ExitStack()
    with ctx:
        def sb(name, shape, dt):
            return ctx.enter_context(nc.sbuf_tensor(name, shape, dt))

        def sem(name):
            return ctx.enter_context(nc.semaphore(name))

        w_hi = sb("w_hi", [P, NC, 2 * D], f32r)
        w_lo = sb("w_lo", [P, NC, 2 * D], f32r)
        w_stage = sb("w_stage", [P, 2, 2 * D], f32)
        x = [sb(f"x{b}", [P, NT, D], f32) for b in range(2)]
        x_hi = [sb(f"x_hi{b}", [P, NT, DX], f32r) for b in range(2)]
        x_lo = [sb(f"x_lo{b}", [P, NT, DX], f32r) for b in range(2)]
        mask_src = [sb(f"mask_src{b}", [P, NT, N], u8) for b in range(2)]
        mask_dst = [sb(f"mask_dst{b}", [P, NT, N], u8) for b in range(2)]
        s = [sb(f"s{b}", [P, NT, 3], f32) for b in range(2)]
        adj_stage = sb("adj_stage", [P, N], i32)
        mask_bf = sb("mask_bf", [P, 2, N], bf16)
        sj_row = sb("sj_row", [P, N], f32)
        r_rows = sb("r_rows", [P, 2, HALF], f32)
        e1 = sb("e1", [P, NE, HALF], f32)
        e2 = sb("e2", [P, 2, HALF], f32)
        y1 = sb("y1", [P, HT, D], f32)
        hT = sb("hT", [P, KD, HALF], f32)
        hT_hi = sb("hT_hi", [P, KD, HALF], f32r)
        hT_lo = sb("hT_lo", [P, KD, HALF], f32r)
        g = sb("g", [P, 2, HALF], f32)
        ring_hi = sb("ring_hi", [P, NR, HALF], f32r)
        ring_lo = sb("ring_lo", [P, NR, HALF], f32r)
        n2 = sb("n2", [P, HT, D], f32)
        x_first = sb("x_first", [P, HT, D], f32)
        w_row = sb("w_row", [P, 2, D], f32)
        g2_row = sb("g2_row", [P, D], f32)
        beta2_row = sb("beta2_row", [P, D], f32)
        b1_col = sb("b1_col", [P, L, NC], f32)
        b2_parts = sb("b2_parts", [BR + 1, L, D], f32r)
        pick_parts = sb("pick_parts", [BR + 1, P], f32r)
        shifted_eye = sb("shifted_eye", [P, 3 * P], f32r)
        g1_col = sb("g1_col", [P, L, KD], f32)
        beta1_col = sb("beta1_col", [P, L, KD], f32)
        attn_b_col = sb("attn_b_col", [P, L], f32)
        ident = sb("ident", [P, P], f32)
        ident_bf = sb("ident_bf", [P, P], bf16)
        eye = sb("eye", [P, P], i32)
        bn1 = sb("bn1", [P, HT, 6], f32)
        mv1 = sb("mv1", [P, HT, 2], f32)
        rstd1 = sb("rstd1", [P, HT], f32)
        bn2 = sb("bn2", [P, HT, 6], f32)
        mv2 = sb("mv2", [P, HT, 2], f32)
        rstd2 = sb("rstd2", [P, HT], f32)
        power = sb("power", [P, HT], f32)
        neg_mean = sb("neg_mean", [P, HT], f32)
        var_eps = sb("var_eps", [P, HT], f32)
        shift1 = sb("shift1", [P, HT], f32)
        shift2 = sb("shift2", [P, HT], f32)
        gate_cell = sb("gate_cell", [P, 1], f32)
        table_cell = sb("table_cell", [P, 2], f32)
        r_sum = sb("r_sum", [P, HT], f32)
        neg_s = sb("neg_s", [P, 2], f32)
        neg_min = sb("neg_min", [P, 1], f32)
        sj_max = sb("sj_max", [P, HT], f32)
        z0 = sb("z0", [P, HT], f32)
        zm = sb("zm", [P, HT], f32)
        row_max = sb("row_max", [P, HT], f32)
        r_col = sb("r_col", [P, 2, HT], f32)

        agg = ctx.enter_context(nc.psum_tensor("agg", [P, 4, 512], f32))
        ff1 = ctx.enter_context(nc.psum_tensor("ff1", [P, 2, 512], f32))
        ff2 = ctx.enter_context(nc.psum_tensor("ff2", [P, 2, 512], f32))

        params_in = sem("params_in")
        rows_in = sem("rows_in")
        cols_in = sem("cols_in")
        x_in = sem("x_in")
        x0_in = sem("x0_in")
        adj_in = [sem(f"adj_in{q}") for q in range(2)]
        w_in = [sem(f"w_in{q}") for q in range(2)]
        out_done = sem("out_done")
        b2_hi_ready = sem("b2_hi_ready")
        b2_lo_ready = sem("b2_lo_ready")
        consts = sem("consts")
        diag_added = sem("diag_added")
        mask_ready = sem("mask_ready")
        dst_ready = sem("dst_ready")
        mask_turned = sem("mask_turned")
        src_ready = sem("src_ready")
        w_split_hi = sem("w_split_hi")
        w_split = sem("w_split")
        x_hi_ready = sem("x_hi_ready")
        x_lo_ready = sem("x_lo_ready")
        s_ready = sem("s_ready")
        sj_turned = sem("sj_turned")
        sj_copied = sem("sj_copied")
        cols_ready = sem("cols_ready")
        r_turned = sem("r_turned")
        r_copied = sem("r_copied")
        exps = sem("exps")
        maxed = sem("maxed")
        p_hi_ready = sem("p_hi_ready")
        p_hi_act_ready = sem("p_hi_act_ready")
        p_lo_ready = sem("p_lo_ready")
        agg_done = sem("agg_done")
        agg_read = sem("agg_read")
        stats1 = sem("stats1")
        rstd1_ready = sem("rstd1_ready")
        n1_ready = sem("n1_ready")
        n1_turned = sem("n1_turned")
        hT_ready = sem("hT_ready")
        hT_hi_ready = sem("hT_hi_ready")
        hT_lo_ready = sem("hT_lo_ready")
        ff1_done = sem("ff1_done")
        gelus = sem("gelus")
        g_hi_ready = sem("g_hi_ready")
        g_lo_ready = sem("g_lo_ready")
        ff2_done = sem("ff2_done")
        neg_s_ready = sem("neg_s_ready")
        neg_s_turned = sem("neg_s_turned")
        neg_min_ready = sem("neg_min_ready")
        stats2 = sem("stats2")
        rstd2_ready = sem("rstd2_ready")
        n2_ready = sem("n2_ready")
        x_ready = sem("x_ready")
        x2_ready = sem("x2_ready")
        masked = sem("masked")
        stats3 = sem("stats3")
        rstd3_ready = sem("rstd3_ready")
        out_ready = sem("out_ready")
        dve_link = sem("dve_link")
        pool_link = sem("pool_link")

        class Links:
            def __init__(self, eng, own, per_round):
                self.eng, self.own, self.per_round, self.n, self.round = eng, own, per_round, 0, None

            def after(self, ins):
                self.n += 1
                ins.then_inc(self.own, 1)
                self.eng.wait_ge(self.own, self.n if self.round is None
                                 else self.round * self.per_round + self.n)

        def masks_before(i, k):
            return 16 if i is None else i * 16 + (16 + 4 * (k - 8))

        def x_count(i, kk):
            if i is None:
                return kk // 2 + 1
            return i * 10 + {1: 2, 2: 4, 3: 6, 4: 8, 5: 10, 6: 11}[kk // 2]

        def stage(q):
            return adj_stage[:, :] if q == 0 else x_first[:, :, :].rearrange("p t d -> p (t d)").bitcast(i32)

        def loop_tiles(i, k):
            return masks_before(i, k) - NT

        def hi_by_act(k, j):
            return k is not None and k < 8 and j > 0 and j % 2 == 0

        def wait_p_hi(eng, i, k, a, j):
            if hi_by_act(k, j):
                eng.wait_ge(p_hi_act_ready, i * 24 + k * 3 + j // 2)
            elif k is None:
                eng.wait_ge(p_hi_ready, a * NT + j + 1)
            elif k < 8:
                eng.wait_ge(p_hi_ready, i * 72 + 16 + k * 5 + (j + 1) // 2 + 1)
            else:
                eng.wait_ge(p_hi_ready, i * 72 + 56 + (k - 8) * NT + j + 1)

        def wait_ring(eng, k, a, j):
            if j >= NR:
                eng.wait_ge(agg_done, a * NT + j - NR + 1)
            elif k is not None:
                eng.wait_ge(ff2_done, (a - 2) * NC + NC + j - NR + 1)

        def chunk_slot(k, c):
            return (k * (NC + NT) + c) % NR

        def prob_slot(k, j):
            return j % NR if k is None else (k * (NC + NT) + NC + j) % NR

        assert STEPS * (NC + NT) % NR == 0

        def last_count(i, k):
            return i * 4 + k - 6

        def feed_slot(k):
            return (k // 2) % 2, k % 2, k // 4

        def attend_slot(k):
            return (k // 2) % 2, k % 2, (k // 4) % L

        block = ctx.enter_context(nc.Block())

        @block.sync
        def _(sp):
            def load_rows(score_layer, norm_layer):
                sp.dma_start(w_row[:, :, :], attn_w[score_layer, :].rearrange("(a c) -> a c", a=2)
                             .partition_broadcast(P)).then_inc(rows_in, 16)
                sp.dma_start(g2_row[:, :], g2[norm_layer, :].partition_broadcast(P)).then_inc(rows_in, 16)
                sp.dma_start(beta2_row[:, :], beta2[norm_layer, :].partition_broadcast(P)).then_inc(rows_in, 16)

            def load_chunk(layer, c, n_split):
                if n_split is not None:
                    sp.wait_ge(w_split, n_split)
                sp.dma_start(w_stage[:, c % 2, 0:D].rearrange("p (k n) -> p k n", k=KD),
                             W1[layer, :, c * P:(c + 1) * P].rearrange("(k p) n -> p k n", p=P)).then_inc(w_in[c % 2], 16)
                sp.dma_start(w_stage[:, c % 2, D:2 * D], W2[layer, c * P:(c + 1) * P, :]).then_inc(w_in[c % 2], 16)

            def load_adj(q, batch, it, first, n_mask):
                if not first:
                    sp.wait_ge(mask_ready, n_mask)
                sp.dma_start(stage(q), adj_d[batch, it * P:(it + 1) * P, :]).then_inc(adj_in[q], 16)

            load_rows(0, 0)
            sp.dma_start(x[0][:, :, :], x_d[0, :, :].rearrange("(t p) d -> p t d", p=P)).then_inc(x_in, 16)
            def first_adj(m):
                load_adj(m % 2, m // NT, m % NT, m < 2, m - 1)

            for m in range(HT):
                first_adj(m)
            sp.dma_start(attn_b_col[:, :], attn_b.partition_broadcast(P)).then_inc(params_in, 16)
            sp.dma_start(n2[0:BR + 1].rearrange("p t d -> p (t d)")[:, 0:L * D],
                         b2.rearrange("l d -> (l d)").partition_broadcast(BR + 1)).then_inc(params_in, 16)
            first_adj(HT)
            first_adj(HT + 1)
            sp.wait_ge(x_in, 16)
            sp.dma_start(x[1][:, :, :], x_d[1, :, :].rearrange("(t p) d -> p t d", p=P)).then_inc(x_in, 16)
            load_chunk(0, 0, None)
            load_chunk(0, 1, None)
            first_adj(HT + 2)
            load_chunk(0, 2, 1)
            load_chunk(0, 3, 2)
            first_adj(HT + 3)
            for dst, src in ((b1_col, b1), (g1_col, g1), (beta1_col, beta1)):
                sp.dma_start(dst[:, :, :], src.rearrange("l (c p) -> p l c", p=P),
                             allow_slow_non_contiguous=True).then_inc(cols_in, 16)
            first_adj(NT)
            first_adj(NT + 1)
            load_chunk(0, 4, 3)
            load_chunk(0, 5, 4)
            for m in range(NT + 2, 2 * NT):
                first_adj(m)
            sp.wait_ge(mask_ready, 2 * NT)
            sp.dma_start(x_first[:, :, :], x_d[0, 0:HALF, :].rearrange("(t p) d -> p t d", p=P)).then_inc(x0_in, 16)

            def store(pair, i, k):
                sp.wait_ge(out_ready, last_count(i, k))
                sp.dma_start(out_d[pair * 2 + (k - 8) // 2, (k % 2) * HALF:(k % 2 + 1) * HALF, :]
                             .rearrange("(t p) d -> p t d", p=P), n2[:, :, :]).then_inc(out_done, 16)

            def pair(i, last):
                nxt = i + 1
                for k in range(STEPS):
                    t = i * STEPS + k
                    b, h, layer = feed_slot(k)

                    def adj_tile(q):
                        load_adj(0, nxt * 2 + (k - 8) // 2, (k % 2) * 4 + q, False, masks_before(i, k) + q)

                    def next_chunk(c):
                        load_chunk((layer + 1) % L, c, i * (L * NC) + (layer + 1) * NC + c - 1)

                    if k >= 8 and not last:
                        adj_tile(0)
                    if k % 4 == 0:
                        for c in (6, 7):
                            load_chunk(layer, c, i * (L * NC) + layer * NC + c - 1)
                    if k == 0:
                        store((i + PAIRS - 1) % PAIRS, i - 1, 11)
                        load_rows(1, 0)

                    if k in (4, 8):
                        sp.wait_ge(s_ready, i * 10 + k + 2)
                        load_rows({4: 2, 8: 0}[k], layer)
                    if k == 11 and not last:
                        next_chunk(0)
                        next_chunk(1)
                    if k >= 8 and not last:
                        adj_tile(1)
                    if k == 11 and not last:
                        next_chunk(2)
                    if k > 8:
                        store(i, i, k - 1)
                    if k in (8, 10) and not last:
                        sp.wait_ge(agg_read, t + 2)
                        sp.dma_start(x[b][:, :, :], x_d[nxt * 2 + b, :, :]
                                     .rearrange("(t p) d -> p t d", p=P)).then_inc(x_in, 16)
                    if k % 4 == 3 and not (last and k == 11):
                        for c in range(3 if k == 11 else 0, 4):
                            next_chunk(c)
                    if k >= 8:
                        if not last:
                            adj_tile(2)
                        sp.dma_start(x_first[:, :, :], x_d[i * 2 + b, h * HALF:(h + 1) * HALF, :]
                                     .rearrange("(t p) d -> p t d", p=P)).then_inc(x0_in, 16)
                    if k % 4 == 3 and not (last and k == 11):
                        next_chunk(4)
                        next_chunk(5)
                    if k >= 8 and not last:
                        adj_tile(3)
            with sp.Fori(0, PAIRS - 1) as i:
                pair(i, False)
            pair(PAIRS - 1, True)
            store(PAIRS - 1, PAIRS - 1, 11)
            sp.wait_ge(out_done, 16 * (B * 2 + 1))
            sp.wait_ge(rows_in, 48 * (1 + 3 * PAIRS))

        @block.gpsimd
        def _(pool):
            links = Links(pool, pool_link, (2 + 1) * STEPS + 4)
            eng = nc.gpsimd

            def split_lo(dst, value, hi, ready):
                eng.tensor_tensor(dst, value, hi.bitcast(f32), ALU.subtract).then_inc(ready, 1)

            def mask_tile(q, it, n_in):
                pool.wait_ge(adj_in[q], n_in * 16)
                d = stage(q)[:, it * P:(it + 1) * P]
                eng.tensor_tensor(d, d, eye[:, :], ALU.add).then_inc(diag_added, 1)

            def inv_std(dst, shift, stats, n_stats, ready):
                pool.wait_ge(stats, n_stats)
                links.after(eng.tensor_tensor(dst[:, :], var_eps[:, :], power[:, :], ALU.pow))
                eng.tensor_tensor(shift[:, :], neg_mean[:, :], dst[:, :], ALU.mult).then_inc(ready, 1)

            def new_batch_lo(b, n):
                pool.wait_ge(x_hi_ready, n)
                split_lo(x_lo[b][:, :, 0:D], x[b][:, :, :], x_hi[b][:, :, 0:D], x_lo_ready)

            def new_half_lo(b, n, part):
                rows = slice(part * HT, (part + 1) * HT)
                pool.wait_ge(x_hi_ready, n)
                ins = eng.tensor_tensor(x_lo[b][:, rows, 0:D], x[b][:, rows, :],
                                        x_hi[b][:, rows, 0:D].bitcast(f32), ALU.subtract)
                if part == 1:
                    ins.then_inc(x_lo_ready, 1)

            def late_part(i, k):
                b, h, layer = feed_slot(k)
                rows = slice(h * HT, (h + 1) * HT)
                if layer < L - 1:
                    pool.wait_ge(x_hi_ready, i * 10 + k + 3)
                    split_lo(x_lo[b][:, rows, 0:D], x[b][:, rows, :], x_hi[b][:, rows, 0:D], x_lo_ready)
                else:
                    inv_std(rstd2, shift2, stats3, last_count(i, k), rstd3_ready)

            def chunk_lo(c, n):
                pool.wait_ge(w_split_hi, n)
                split_lo(w_lo[:, c, :], w_stage[:, c % 2], w_hi[:, c, :], w_split)

            def prob_lo(i, k, a, j):
                r = prob_slot(k, j)
                wait_p_hi(pool, i, k, a, j)
                split_lo(ring_lo[:, r], e1[:, j % NE], ring_hi[:, r], p_lo_ready)

            eng.memset(power[:, :], -0.5)
            for b in range(2):
                eng.memset(x_hi[b][:, :, D:D + 1].bitcast(f32), 1.0)
                eng.memset(x_hi[b][:, :, D + 1:DX].bitcast(f32), 0.0)
                eng.memset(x_lo[b][:, :, D:DX].bitcast(f32), 0.0)
            eng.memset(ident[:, :], 0.0)
            eng.memset(eye[:, :], 0)
            eng.memset(shifted_eye[:, :].bitcast(f32), 0.0)
            links.after(eng.memset(pick_parts[:, :].bitcast(f32), 0.0))
            links.after(eng.memset(pick_parts[0:1, :].bitcast(f32), 1.0))
            links.after(eng.memset(pick_parts[BR:BR + 1, :].bitcast(f32), 1.0))
            links.after(eng.affine_select(out=ident[:, :], in_=ident[:, :], compare_op=ALU.not_equal, fill=1.0, base=0,
                                          pattern=[[-1, P]], channel_multiplier=1))
            eng.tensor_copy(shifted_eye[:, P:2 * P], ident[:, :])
            links.after(eng.tensor_copy(eye[:, :], ident[:, :]))
            eng.tensor_copy(ident_bf[:, :], ident[:, :]).then_inc(consts, 1)
            def first_tile(m):
                mask_tile(m % 2, m % NT, m // 2 + 1)

            for m in range(HT):
                first_tile(m)
            new_batch_lo(0, 1)
            pool.wait_ge(x_lo_ready, 1)
            pool.wait_ge(b2_hi_ready, 1)
            b2_lo = b2_parts[BR:BR + 1].rearrange("p l d -> p (l d)")
            eng.tensor_tensor(b2_lo, n2[BR:BR + 1].rearrange("p t d -> p (t d)")[:, 0:L * D],
                              b2_lo.bitcast(f32), ALU.subtract).then_inc(b2_lo_ready, 1)
            pool.wait_ge(b2_lo_ready, 1)
            eng.memset(n2[:, 0:HT // 2, :], 0.0).then_inc(x_ready, 1)
            for a in range(2):
                first = HT + NT * a
                first_tile(first)
                first_tile(first + 1)
                for j in range(NT):
                    if j in (3, 5):
                        first_tile(first + (j + 1) // 2)
                    prob_lo(None, None, a, j)
                    if a == 0 and j < 4:
                        chunk_lo(j, j + 1)
                if a == 0:
                    first_tile(NT)
                    first_tile(NT + 1)
                    inv_std(rstd1, shift1, stats1, 1, rstd1_ready)
                    first_tile(NT + 2)
                    pool.wait_ge(hT_hi_ready, 1)
                    for kd in range(KD):
                        split_lo(hT_lo[:, kd, :], hT[:, kd, :], hT_hi[:, kd, :], hT_lo_ready)
                    first_tile(NT + 3)
                    new_batch_lo(1, 2)
            n_ahead = links.n

            def pair(i, last):
                links.round, links.n = i, n_ahead
                for k in range(STEPS):
                    t = i * STEPS + k
                    b, h, layer = feed_slot(k)
                    n_chunk = i * (L * NC) + (layer + (1 if k % 4 == 3 else 0)) * NC
                    for c in range(NC):
                        pool.wait_ge(g_hi_ready, t * NC + c + 1)
                        r = chunk_slot(k, c)
                        split_lo(ring_lo[:, r], g[:, c % 2], ring_hi[:, r], g_lo_ready)
                        if c == 0 and not (last and k == 11):
                            inv_std(rstd1, shift1, stats1, t + 2, rstd1_ready)
                        if c == (6 if k % 4 == 0 else 5) and 1 <= k <= 8:
                            late_part(i, k - 1)
                        if k >= 8 and c in (1, 5) and not last:
                            mask_tile(0, (k % 2) * 4 + c // 4, loop_tiles(i, k) + c // 4 + 1)
                        if k in (9, 11) and c in (3, 4) and not last:
                            new_half_lo((k - 8) // 2, i * 10 + {9: 11, 11: 12}[k], c - 3)
                        if c == (4 if h == 1 else 2) and (k == 0 or k > 8):
                            late_part(i - (k == 0), (k - 1) % STEPS)
                        if k % 4 == 3 and 4 <= c < 7 and not (last and k == 11):
                            chunk_lo(c - 4, n_chunk + c - 3)
                        if k % 4 == 0 and c in (1, 2, 4, 5):
                            rest = NC // 2 + (1, 2, 4, 5).index(c)
                            chunk_lo(rest, n_chunk + rest + 1)
                    for j in range(NT):
                        if k >= 8 and j in (3, 5) and not last:
                            q = (j + 1) // 2
                            mask_tile(0, (k % 2) * 4 + q, loop_tiles(i, k) + q + 1)
                        if j < KD and not (last and k == 11):
                            if j == 0:
                                pool.wait_ge(hT_hi_ready, t + 2)
                            split_lo(hT_lo[:, j, :], hT[:, j, :], hT_hi[:, j, :], hT_lo_ready)
                        if not (last and k >= 10):
                            prob_lo(i, k, t + 2, j)
                        if k % 4 == 3 and j == 2 and not (last and k == 11):
                            chunk_lo(3, n_chunk + 4)
                        if j == 4:
                            inv_std(rstd2, shift2, stats2, t + 1, rstd2_ready)
                    pool.wait_ge(n2_ready, t + 2)
                    if k % 4 == 0:
                        pool.wait_ge(rows_in, (i * 3 + 2 + layer) * 48)
                    first = slice(0, HT // 2)
                    g2_t, beta2_t = (r[:, :].unsqueeze(1).broadcast_to([P, HT // 2, D]) for r in (g2_row, beta2_row))
                    links.after(eng.tensor_tensor(n2[:, first, :], n2[:, first, :], g2_t, ALU.mult))
                    dst = x[b][:, h * HT:h * HT + HT // 2, :] if layer < L - 1 else n2[:, first, :]
                    eng.tensor_tensor(dst, n2[:, first, :], beta2_t, ALU.add).then_inc(x_ready, 1)
                if not last:
                    assert links.n - n_ahead == links.per_round

            with pool.Fori(0, PAIRS - 1) as i:
                pair(i, False)
            pair(PAIRS - 1, True)
            late_part(PAIRS - 1, STEPS - 1)

        @block.scalar
        def _(act):
            eng = nc.scalar

            def mask_dst_tile(b, it, n):
                act.wait_ge(mask_ready, n)
                eng.activation(mask_dst[b][:, it, :], mask_bf[:, it % 2, :], ACT.Copy).then_inc(dst_ready, 1)

            def mask_src_tile(b, it, n):
                act.wait_ge(mask_turned, n)
                eng.activation(mask_src[b][:, :, it * P:(it + 1) * P],
                               ff1[:, it % 2, :].bitcast(bf16).rearrange("p (j i) -> p j i", j=NT),
                               ACT.Copy).then_inc(src_ready, 1)

            def sj_copy(n):
                act.wait_ge(sj_turned, n)
                act.wait_ge(neg_min_ready, n)
                eng.activation(sj_row[:, :].rearrange("p (a n) -> p a n", a=2), agg[:, 2:4, :],
                               ACT.Identity, bias=neg_min[:, :], scale=1.0).then_inc(sj_copied, 1)

            def r_copy(a):
                act.wait_ge(r_turned, a + 1)
                eng.activation(r_rows[:, :, :], agg[:, 2:4, :], ACT.Copy).then_inc(r_copied, 1)

            def hT_copy(a, layer):
                act.wait_ge(n1_turned, a + 1)
                for kd in range(KD):
                    ins = eng.activation(hT[:, kd, :], agg[:, kd, :], ACT.Identity,
                                         bias=beta1_col[:, layer, kd:kd + 1], scale=g1_col[:, layer, kd:kd + 1])
                ins.then_inc(hT_ready, 1)

            def normalize(dst, src, rstd, shift, ready, n, done):
                act.wait_ge(ready, n)
                for it in range(HT):
                    ins = eng.activation(dst[:, it, :], src(it), ACT.Identity,
                                         bias=shift[:, it:it + 1], scale=rstd[:, it:it + 1])
                ins.then_inc(done, 1)

            def exp_tile(b, a, j, e1_free, e2_free):
                if e1_free:
                    act.wait_ge(p_lo_ready, a * NT + j - NE + 1)
                if e2_free:
                    act.wait_ge(maxed, a * NT + j - 1)
                if j == 0:
                    act.wait_ge(r_copied, a + 1)
                eng.activation(e1[:, j % NE, :], r_rows[:, 0, :], ACT.Exp, bias=s[b][:, j, 1:2], scale=1.0)
                eng.activation(e2[:, j % 2, :], r_rows[:, 1, :], ACT.Exp, bias=s[b][:, j, 2:3],
                               scale=1.0).then_inc(exps, 1)

            def prob_hi(k, a, j):
                r = prob_slot(k, j)
                act.wait_ge(masked, a * NT + j + 1)
                wait_ring(act, k, a, j)
                eng.activation(ring_hi[:, r], e1[:, j % NE], ACT.Copy).then_inc(p_hi_act_ready, 1)

            def late_part(i, k):
                b, h, layer = feed_slot(k)
                rows = slice(h * HT, (h + 1) * HT)
                if layer < L - 1:
                    act.wait_ge(x_ready, i * STEPS + k + 2)
                    act.wait_ge(x2_ready, i * STEPS + k + 2)
                    eng.activation(x_hi[b][:, rows, 0:D], x[b][:, rows, :], ACT.Copy).then_inc(x_hi_ready, 1)
                else:
                    normalize(n2, lambda it: n2[:, it, :], rstd2, shift2, rstd3_ready, last_count(i, k), out_ready)

            act.wait_ge(x_in, 16)
            eng.activation(x_hi[0][:, :, 0:D], x[0][:, :, :], ACT.Copy).then_inc(x_hi_ready, 1)
            def dst(m):
                mask_dst_tile(m // NT, m % NT, m + 1)

            def src(m):
                mask_src_tile(m // NT, m % NT, m + 1)

            for m in range(HT):
                dst(m)
                src(m)
            act.wait_ge(params_in, 16 * 2)
            sj_copy(1)
            for a in range(2):
                first = HT + NT * a
                dst(first)
                r_copy(a)
                for j in range(NT):
                    exp_tile(0, a, j, a > 0 or j >= NE, a > 0 or j >= 2)
                    if j == 3:
                        dst(first + 1)
                    if j in (4, 5, 7):
                        src(first + {4: 0, 5: 1, 7: 2}[j])
                    if j == 6:
                        dst(first + 2)
                dst(first + 3)
                src(first + 3)
                if a == 0:
                    dst(NT)
                    src(NT)
                    normalize(y1, lambda it: y1[:, it, :], rstd1, shift1, rstd1_ready, 1, n1_ready)
                    dst(NT + 1)
                    src(NT + 1)
                    act.wait_ge(cols_in, 16 * 3)
                    hT_copy(0, 0)
                    for m in (NT + 2, NT + 3):
                        dst(m)
                        src(m)
                    act.wait_ge(x_in, 32)
                    eng.activation(x_hi[1][:, :, 0:D], x[1][:, :, :], ACT.Copy).then_inc(x_hi_ready, 1)

            def pair(i, last):
                for k in range(STEPS):
                    t = i * STEPS + k
                    b, h, layer = feed_slot(k)
                    ab, ah, _l = attend_slot(k + 2)
                    attends = not (last and k >= 10)
                    mb, mt = (k - 8) // 2, (k % 2) * 4
                    for c in range(NC):
                        act.wait_ge(ff1_done, t * NC + c + 1)
                        if c >= 2:
                            act.wait_ge(g_lo_ready, t * NC + c - 1)
                        eng.activation(g[:, c % 2, :], ff1[:, c % 2, :], ACT.Gelu,
                                       bias=b1_col[:, layer, c:c + 1], scale=1.0).then_inc(gelus, 1)
                        if c == 2 and not (last and k == 11):
                            normalize(y1, lambda it: y1[:, it, :], rstd1, shift1, rstd1_ready, t + 2, n1_ready)
                        if c == 3 and ah == 0 and attends:
                            sj_copy(i * (STEPS // 2) + (k + 2) // 2 + 1)
                        if c == (6 if ah == 1 else 4) and (k == 0 or k > 8):
                            late_part(i - (k == 0), (k - 1) % STEPS)
                        if k in (9, 11) and c == 3 and not last:
                            nb = (k - 8) // 2
                            act.wait_ge(x_in, (i * 2 + nb + 3) * 16)
                            eng.activation(x_hi[nb][:, :, 0:D], x[nb][:, :, :], ACT.Copy).then_inc(x_hi_ready, 1)
                        if c == 4 - ah and 1 <= k <= 8:
                            late_part(i, k - 1)
                        if c == 5 and not (last and k == 11):
                            hT_copy(t + 1, ((k + 1) // 4) % L)
                        if c == 6 and attends:
                            r_copy(t + 2)
                        if k >= 8 and c == 5 and not last:
                            mask_dst_tile(mb, mt, masks_before(i, k) + 1)
                    if attends:
                        eng.activation(table_cell[:, 0:1], ident[:, 0:1], ACT.Exp)
                        if ah == 1 and not (last and k == 9):
                            act.wait_ge(s_ready, i * 10 + {9: 11, 11: 12}.get(k, k + 2))
                        for j in range(NT):
                            exp_tile(ab, t + 2, j, True, True)
                            if k >= 8 and j == 3 and not last:
                                mask_dst_tile(mb, mt + 1, masks_before(i, k) + 2)
                            if k < 8 and j in (4, 6, 7):
                                prob_hi(k, t + 2, {4: 2, 6: 4, 7: 6}[j])
                            if k >= 8 and j in (4, 5, 7) and not last:
                                q = {4: 0, 5: 1, 7: 2}[j]
                                mask_src_tile(mb, mt + q, masks_before(i, k) + q + 1)
                            if k >= 8 and j == 6 and not last:
                                mask_dst_tile(mb, mt + 2, masks_before(i, k) + 3)
                        eng.activation(table_cell[:, 1:2], ident[:, 0:1], ACT.Gelu)
                    if k == 0 or k > 8:
                        act.wait_ge(out_done, last_count(i - (k == 0), (k - 1) % STEPS) * 16)
                    normalize(n2, lambda it: ff2[:, it // 2, (it % 2) * D:(it % 2 + 1) * D], rstd2, shift2,
                              rstd2_ready, t + 1, n2_ready)
                    if k >= 8 and not last:
                        mask_src_tile(mb, mt + 3, masks_before(i, k) + 4)
                        mask_dst_tile(mb, mt + 3, masks_before(i, k) + 4)
            with act.Fori(0, PAIRS - 1) as i:
                pair(i, False)
            pair(PAIRS - 1, True)
            late_part(PAIRS - 1, STEPS - 1)

        @block.vector
        def _(dve):
            eng = nc.vector
            links = Links(dve, dve_link, STEPS * (1 + 2 + 2 + HT // 2 + 3 + 1) + STEPS // 2 + (L - 1) * 4 * HT
                          + 4 * (1 + 2) + 2 * NT)

            def gate():
                eng.memset(gate_cell[:, :], 0.0)

            def mask_tile(st, q, n, first):
                dve.wait_ge(diag_added, n)
                if not first:
                    dve.wait_ge(dst_ready, n - 2)
                    dve.wait_ge(mask_turned, n - 2)
                eng.tensor_scalar(mask_bf[:, q, :], stage(st), 0.0, None, ALU.is_gt).then_inc(mask_ready, 1)

            def scores(b, tiles, end=True):
                for it in tiles:
                    for side in range(2):
                        ins = eng.tensor_tensor_reduce(
                            out=e2[:, side, 0:D // 2].bitcast(bf16), in0=x[b][:, it, :], in1=w_row[:, side, :], scale=1.0,
                            scalar=0.0, op0=ALU.mult, op1=ALU.add, accum_out=s[b][:, it, side:side + 1])
                    links.after(ins)
                sl = slice(tiles[0], tiles[-1] + 1)
                ins = eng.tensor_scalar(s[b][:, sl, 2], s[b][:, sl, 1], SLOPE, None, ALU.mult)
                if end:
                    ins.then_inc(s_ready, 1)

            def chunk_hi(c, n):
                dve.wait_ge(w_in[c % 2], n * 32)
                eng.tensor_copy(w_hi[:, c, :], w_stage[:, c % 2]).then_inc(w_split_hi, 1)

            def minus_min_columns(b):
                links.after(eng.tensor_reduce(out=neg_s[:, 0:1], in_=s[b][:, :, 1], axis=AX.X, op=ALU.min))
                eng.tensor_scalar(neg_s[:, 1:2], neg_s[:, 0:1], -1.0, None, ALU.mult).then_inc(neg_s_ready, 1)

            def minus_min(n):
                dve.wait_ge(neg_s_turned, n)
                eng.tensor_reduce(out=neg_min[:, :], in_=agg[:, 0, 0:P], axis=AX.X, op=ALU.max).then_inc(neg_min_ready, 1)

            def row_maxima(b, its):
                for it in its:
                    ins = eng.tensor_tensor_reduce(
                        out=e2[:, it % 2, :].bitcast(bf16), in0=sj_row[:, :], in1=mask_dst[b][:, it, :], scale=1.0, scalar=0.0,
                        op0=ALU.mult, op1=ALU.max, accum_out=sj_max[:, it % HT:it % HT + 1])
                    if it % 2 == 1:
                        links.after(ins)
                        gate()

            def shift_columns(b, h, layer):
                si = s[b][:, h * HT:(h + 1) * HT, 0]
                links.after(eng.tensor_scalar(z0[:, :], si, attn_b_col[:, layer:layer + 1], None, ALU.add))
                links.after(eng.scalar_tensor_tensor(out=zm[:, :], in0=sj_max[:, :], scalar=neg_min[:, :],
                                                     in1=z0[:, :], op0=ALU.subtract, op1=ALU.add))
                links.after(eng.scalar_tensor_tensor(out=row_max[:, :], in0=zm[:, :], scalar=SLOPE,
                                                     in1=zm[:, :], op0=ALU.mult, op1=ALU.max))
                eng.tensor_tensor(r_col[:, 0, :], z0[:, :], row_max[:, :], ALU.subtract)
                eng.scalar_tensor_tensor(out=r_col[:, 1, :], in0=z0[:, :], scalar=SLOPE, in1=row_max[:, :],
                                         op0=ALU.mult, op1=ALU.subtract).then_inc(cols_ready, 1)

            def probs(b, h, k, a, tiles):
                def hi(j):
                    if hi_by_act(k, j):
                        return
                    dve.wait_ge(masked, a * NT + j + 1)
                    wait_ring(dve, k, a, j)
                    eng.tensor_copy(ring_hi[:, prob_slot(k, j), :], e1[:, j % NE, :]).then_inc(p_hi_ready, 1)

                for j in tiles:
                    e = e1[:, j % NE, :]
                    dve.wait_ge(exps, a * NT + j + 1)
                    eng.tensor_tensor(e, e, e2[:, j % 2, :], ALU.max).then_inc(maxed, 1)
                    if j > 1:
                        hi(j - 1)
                    dve.wait_ge(maxed, a * NT + j + 1)
                    eng.tensor_tensor(e, e, mask_src[b][:, j, h * HALF:(h + 1) * HALF], ALU.min).then_inc(masked, 1)
                    if j == 0:
                        hi(0)
                if tiles[-1] == NT - 1:
                    hi(NT - 1)

            def residual1(b, h, a):
                dve.wait_ge(agg_done, a * NT + NT)
                for it in range(HT):
                    ins = eng.reciprocal(r_sum[:, it:it + 1], agg[:, it, D:D + 1])
                links.after(ins)
                for it in range(HT):
                    ins = eng.scalar_tensor_tensor(out=y1[:, it, :], in0=agg[:, it, 0:D], scalar=r_sum[:, it:it + 1],
                                                   in1=x[b][:, h * HT + it, :], op0=ALU.mult, op1=ALU.add)
                ins.then_inc(agg_read, 1)
                dve.wait_ge(agg_read, a + 1)

            def mean_var(src, bn, mv, ready, used, used_n):
                for it in range(HT):
                    ins = eng.bn_stats(bn[:, it, :], src(it))
                links.after(ins)
                gate()
                for it in range(HT):
                    ins = eng.bn_aggr(mv[:, it, :], bn[:, it, :])
                links.after(ins)
                if used_n is not None:
                    dve.wait_ge(used, used_n)
                eng.tensor_scalar(var_eps[:, :], mv[:, :, 1], EPS, None, ALU.add)
                eng.tensor_scalar(neg_mean[:, :], mv[:, :, 0], -1.0, None, ALU.mult).then_inc(ready, 1)

            def hT_split(a):
                dve.wait_ge(hT_ready, a + 1)
                eng.tensor_copy(hT_hi[:, :, :], hT[:, :, :]).then_inc(hT_hi_ready, 1)

            def late_scaling(i, k):
                b, h, layer = feed_slot(k)
                dve.wait_ge(n2_ready, i * STEPS + k + 2)
                if k % 4 == 0:
                    dve.wait_ge(rows_in, (i * 3 + 2 + layer) * 48)
                last = slice(HT // 2, HT)
                g2_t, beta2_t = (r[:, :].unsqueeze(1).broadcast_to([P, HT // 2, D]) for r in (g2_row, beta2_row))
                links.after(eng.tensor_tensor(n2[:, last, :], n2[:, last, :], g2_t, ALU.mult))
                dst = x[b][:, h * HT + HT // 2:(h + 1) * HT, :] if layer < L - 1 else n2[:, last, :]
                eng.tensor_tensor(dst, n2[:, last, :], beta2_t, ALU.add).then_inc(x2_ready, 1)

            def late_rest(i, k, *used_by):
                b, h, layer = feed_slot(k)
                dve.wait_ge(x2_ready, i * STEPS + k + 2)
                dve.wait_ge(x_ready, i * STEPS + k + 2)
                if layer < L - 1:
                    scores(b, range(h * HT, (h + 1) * HT))
                else:
                    dve.wait_ge(x0_in, last_count(i, k) * 16)
                    links.after(eng.tensor_tensor(n2[:, :, :], n2[:, :, :], x_first[:, :, :], ALU.add))
                    mean_var(lambda it: n2[:, it, :], bn2, mv2, stats3, *used_by)

            eng.memset(bn2[:, 0, :], 0.0).then_inc(n2_ready, 1)
            dve.wait_ge(rows_in, 48)
            def first_tile(m):
                mask_tile(m % 2, m % 2, m + 1, m < 2)

            for m in range(HT):
                first_tile(m)
                if m == 0:
                    dve.wait_ge(x_in, 16)
                scores(0, range(2 * m, 2 * m + 2), end=(m == HT - 1))
            minus_min_columns(0)
            dve.wait_ge(params_in, 16 * 2)
            eng.tensor_copy(b2_parts[:, :, :].rearrange("p l d -> p (l d)"),
                            n2[0:BR + 1].rearrange("p t d -> p (t d)")[:, 0:L * D]).then_inc(b2_hi_ready, 1)
            minus_min(1)
            dve.wait_ge(src_ready, HT)
            dve.wait_ge(sj_copied, 1)
            for a in range(2):
                first = HT + NT * a
                dve.wait_ge(dst_ready, HT + HT * a)
                row_maxima(0, range(HT * a, HT * a + HT))
                shift_columns(0, a, 0)
                if a == 1:
                    first_tile(NT + 2)
                    hT_split(0)
                    first_tile(NT + 3)
                first_tile(first)
                first_tile(first + 1)
                dve.wait_ge(src_ready, HT + HT * a)
                for j in range(NT):
                    probs(0, a, None, a, [j])
                    if j in (4, 6):
                        first_tile(first + j // 2)
                    if a == 0 and j < 4:
                        chunk_hi(j, j // 2 + 1)
                if a == 1:
                    dve.wait_ge(n1_turned, 1)
                residual1(0, a, a)
                if a == 0:
                    mean_var(lambda it: y1[:, it, :], bn1, mv1, stats1, None, None)
                    first_tile(NT)
                    first_tile(NT + 1)
                    dve.wait_ge(b2_lo_ready, 1)
                    eng.memset(n2[:, HT // 2:HT, :], 0.0).then_inc(x2_ready, 1)
                else:
                    dve.wait_ge(x_in, 32)
                    scores(1, range(NT))
            n_ahead = links.n

            def pair(i, last):
                links.round, links.n = i, n_ahead
                for k in range(STEPS):
                    t = i * STEPS + k
                    b, h, layer = feed_slot(k)
                    ab, ah, al = attend_slot(k + 2)
                    attends = not (last and k >= 10)
                    norms = not (last and k == 11)
                    new_weights = k % 4 == 3 and norms
                    n_norm = t + 2 if norms else t + 1

                    def gelu_hi(c):
                        dve.wait_ge(gelus, t * NC + c + 1)
                        if c >= NR:
                            dve.wait_ge(ff2_done, t * NC + c - NR + 1)
                        eng.tensor_copy(ring_hi[:, chunk_slot(k, c)], g[:, c % 2]).then_inc(g_hi_ready, 1)

                    def next_hi(c):
                        dve.wait_ge(ff2_done, t * NC + c + 1)
                        chunk_hi(c, i * (L * NC // 2) + ((layer + 1) * NC + c) // 2 + 1)

                    def rest_hi(c):
                        chunk_hi(c, i * (L * NC // 2) + (layer * NC + c) // 2 + 1)

                    def masks(q):
                        mask_tile(0, q % 2, masks_before(i, k) + q + 1, False)

                    def late():
                        late_rest(i - (k == 0), (k - 1) % STEPS, rstd1_ready, n_norm)

                    def maxima(half):
                        row_maxima(ab, range(ah * HT + half * 2, ah * HT + half * 2 + 2))

                    n_sj = i * (STEPS // 2) + (k + 2) // 2 + 1
                    nb = (k - 8) // 2
                    gelu_hi(0)
                    if norms:
                        mean_var(lambda it: y1[:, it, :], bn1, mv1, stats1, rstd1_ready, t + 1)
                    gelu_hi(1)
                    if ah == 0:
                        if k in (0, 10):
                            if attends:
                                minus_min_columns(ab)
                            if k == 0:
                                rest_hi(4)
                                rest_hi(5)
                            late()
                        else:
                            late()
                            if attends:
                                minus_min_columns(ab)
                            if k % 4 == 0:
                                rest_hi(4)
                                rest_hi(5)
                    elif attends:
                        maxima(0)
                    gelu_hi(2)
                    if k >= 8 and not last:
                        masks(0)
                    if attends:
                        if ah == 1:
                            maxima(1)
                        else:
                            minus_min(n_sj)
                    gelu_hi(3)
                    if attends:
                        if ah == 1:
                            shift_columns(ab, ah, al)
                        else:
                            if k + 2 == STEPS:
                                dve.wait_ge(dst_ready, masks_before(i, 10))
                            if k + 2 == 2:
                                dve.wait_ge(dst_ready, masks_before(i, 8))
                            dve.wait_ge(sj_copied, n_sj)
                            gate()
                            maxima(0)
                    if k in (9, 11) and not last:
                        dve.wait_ge(x_in, (i * 2 + nb + 3) * 16)
                        dve.wait_ge(rows_in, (i * 3 + 4) * 48)
                        scores(nb, range(0, 2), end=False)
                    gelu_hi(4)
                    if k % 4 == 0:
                        rest_hi(6)
                    if ah == 1:
                        late()
                    elif attends:
                        maxima(1)
                        shift_columns(ab, ah, al)
                    if new_weights:
                        next_hi(0)
                    gelu_hi(5)
                    if k % 4 == 0:
                        rest_hi(7)
                    if k in (9, 11) and not last:
                        scores(nb, range(2, 5), end=False)
                    if new_weights:
                        next_hi(1)
                    gelu_hi(6)
                    if k in (9, 11) and not last:
                        scores(nb, range(5, NT))
                    if new_weights:
                        next_hi(2)
                    gelu_hi(7)
                    if norms:
                        dve.wait_ge(ff1_done, t * NC + NC)
                        hT_split(t + 1)
                    if k >= 8 and not last:
                        masks(1)

                    for j in range(NT):
                        if attends:
                            probs(ab, ah, k, t + 2, [j])
                        if new_weights and j == 1:
                            next_hi(3)
                        if k >= 8 and j in (4, 6) and not last:
                            masks(j // 2)
                        if j == 3:
                            dve.wait_ge(ff2_done, t * NC + NC)
                            mean_var(lambda it: ff2[:, it // 2, (it % 2) * D:(it % 2 + 1) * D], bn2, mv2, stats2, rstd1_ready, n_norm)
                    late_scaling(i, k)
                    if attends:
                        residual1(ab, ah, t + 2)
                if not last:
                    assert links.n - n_ahead == links.per_round

            with dve.Fori(0, PAIRS - 1) as i:
                pair(i, False)
            pair(PAIRS - 1, True)
            late_rest(PAIRS - 1, STEPS - 1, rstd2_ready, PAIRS * STEPS)

        @block.tensor
        def _(pe):
            eng = nc.tensor

            def mask_tile(it, n, first):
                pe.wait_ge(mask_ready, n)
                if not first:
                    pe.wait_ge(src_ready, n - 2)
                bank = ff1[:, it % 2, :].bitcast(bf16)
                for j in range(NT):
                    ins = eng.transpose(bank[:, j * P:(j + 1) * P], mask_bf[:, it % 2, j * P:(j + 1) * P], ident_bf[:, :])
                ins.then_inc(mask_turned, 1)

            def sj_turn(b, n_s, n_sj, n_agg):
                pe.wait_ge(s_ready, n_s)
                if n_agg is not None:
                    pe.wait_ge(agg_read, n_agg)
                pe.wait_ge(neg_s_ready, n_sj)
                eng.transpose(agg[:, 0, 0:P], neg_s[:, 1:2].to_broadcast([P, P]), ident[:, :]).then_inc(neg_s_turned, 1)
                for j in range(NT):
                    ins = eng.transpose(agg[:, 2 + j // 4, (j % 4) * P:(j % 4 + 1) * P],
                                        s[b][:, j, 1:2].to_broadcast([P, P]), ident[:, :])
                ins.then_inc(sj_turned, 1)

            def r_turn(a, n_sj, n_agg):
                pe.wait_ge(cols_ready, a + 1)
                pe.wait_ge(sj_copied, n_sj)
                if n_agg is not None:
                    pe.wait_ge(agg_read, n_agg)
                for r in range(2):
                    for it in range(HT):
                        ins = eng.transpose(agg[:, 2 + r, it * P:(it + 1) * P],
                                            r_col[:, r, it:it + 1].to_broadcast([P, P]), ident[:, :])
                ins.then_inc(r_turned, 1)

            def aggregate(b, i, k, a, jt, n_x, first_step):
                r = prob_slot(k, jt)
                if jt == 0:
                    pe.wait_ge(r_copied, a + 1)
                    pe.wait_ge(x_lo_ready, n_x)
                    if not first_step:
                        pe.wait_ge(hT_ready, a)
                wait_p_hi(pe, i, k, a, jt)
                for it in range(HT):
                    hi = ring_hi[:, r, it * P:(it + 1) * P]
                    eng.matmul(agg[:, it, 0:DX], hi, x_lo[b][:, jt, :], start=(jt == 0), stop=False)
                    eng.matmul(agg[:, it, 0:DX], hi, x_hi[b][:, jt, :], start=False, stop=False)
                pe.wait_ge(p_lo_ready, a * NT + jt + 1)
                for it in range(HT):
                    lo = ring_lo[:, r, it * P:(it + 1) * P]
                    ins = eng.matmul(agg[:, it, 0:DX], lo, x_hi[b][:, jt, :], start=False, stop=(jt == NT - 1))
                ins.then_inc(agg_done, 1)

            def n1_turn(a):
                pe.wait_ge(n1_ready, a + 1)
                for kd in range(KD):
                    for it in range(HT):
                        ins = eng.transpose(agg[:, kd, it * P:(it + 1) * P], y1[:, it, kd * P:(kd + 1) * P], ident[:, :])
                ins.then_inc(n1_turned, 1)

            def hidden(t, c):
                if c == 0:
                    pe.wait_ge(hT_lo_ready, (t + 1) * KD)
                if c >= 2:
                    pe.wait_ge(gelus, t * NC + c - 1)
                for kd in range(KD):
                    whi, wlo = w_hi[:, c, kd * P:(kd + 1) * P], w_lo[:, c, kd * P:(kd + 1) * P]
                    eng.matmul(ff1[:, c % 2, :], wlo, hT_hi[:, kd, :], start=(kd == 0), stop=False)
                    eng.matmul(ff1[:, c % 2, :], whi, hT_hi[:, kd, :], start=False, stop=False)
                    ins = eng.matmul(ff1[:, c % 2, :], whi, hT_lo[:, kd, :], start=False, stop=(kd == KD - 1))
                ins.then_inc(ff1_done, 1)

            def ff2_rows(it):
                return ff2[:, it // 2, (it % 2) * D:(it % 2 + 1) * D]

            def output_start(t, layer):
                pe.wait_ge(n2_ready, t + 1)
                for a in range(HT // 2):
                    eng.matmul(ff2[:, a, :].rearrange("p (r d) -> p r d", r=2), pick_parts[:, :],
                               b2_parts[:, layer, :].unsqueeze(1).broadcast_to([BR + 1, 2, D]), start=True, stop=False)
                for it in range(HT):
                    for kd in range(KD):
                        for part in (hT_lo, hT_hi):
                            eng.matmul(ff2_rows(it), part[:, kd, it * P:(it + 1) * P],
                                       shifted_eye[:, (1 - kd) * P:(3 - kd) * P], start=False, stop=False)

            def output(k, t, c):
                r = chunk_slot(k, c)
                whi, wlo = w_hi[:, c, D:2 * D], w_lo[:, c, D:2 * D]
                pe.wait_ge(g_hi_ready, t * NC + c + 1)
                for it in range(HT):
                    hi = ring_hi[:, r, it * P:(it + 1) * P]
                    eng.matmul(ff2_rows(it), hi, wlo, start=False, stop=False)
                    eng.matmul(ff2_rows(it), hi, whi, start=False, stop=False)
                pe.wait_ge(g_lo_ready, t * NC + c + 1)
                for it in range(HT):
                    lo = ring_lo[:, r, it * P:(it + 1) * P]
                    ins = eng.matmul(ff2_rows(it), lo, whi, start=False, stop=(c == NC - 1 and it % 2 == 1))
                ins.then_inc(ff2_done, 1)

            pe.wait_ge(consts, 1)
            def first_tile(m):
                mask_tile(m % NT, m + 1, m < 2)

            for m in range(HT):
                first_tile(m)
            sj_turn(0, 1, 1, None)
            for a in range(2):
                first = HT + NT * a
                r_turn(a, 1, a if a else None)
                if a == 1:
                    first_tile(NT + 3)
                for j in range(NT):
                    aggregate(0, None, None, a, j, 1, a == 0)
                    if j in (1, 2, 5, 7):
                        first_tile(first + (1, 2, 5, 7).index(j))
                if a == 0:
                    first_tile(NT)
                    n1_turn(0)
                    first_tile(NT + 1)
                    first_tile(NT + 2)
            pe.wait_ge(b2_lo_ready, 1)

            def pair(i, last):
                for k in range(STEPS):
                    t = i * STEPS + k
                    ab, ah, _l = attend_slot(k + 2)
                    attends = not (last and k >= 10)
                    tail = 4 + ah
                    n_sj = i * (STEPS // 2) + (k + 2) // 2 + 1
                    if k % 4 == 0:
                        pe.wait_ge(w_split, (i * L + k // 4) * NC + NC // 2)
                    for c in range(NC):
                        if c < 2 and (k == 0 or k > 8 and not last):
                            pe.wait_ge(src_ready, masks_before(i, max(k, 8)) - 1 + c)
                        if k % 4 == 0 and c >= NC // 2:
                            pe.wait_ge(w_split, (i * L + k // 4) * NC + c + 1)
                        hidden(t, c)
                        if c == 1:
                            output_start(t, k // 4)
                        if c == 3 and ah == 0 and attends:
                            sj_turn(ab, x_count(i, k + 2), n_sj, t + 2)
                        if 2 <= c < NC - tail + 2:
                            output(k, t, c - 2)
                        if c == 5 and not (last and k == 11):
                            if ah == 0 and attends:
                                pe.wait_ge(neg_min_ready, n_sj)
                            n1_turn(t + 1)
                        if c == 6 - ah and attends:
                            r_turn(t + 2, n_sj, t + 2)
                    for c in range(NC - tail, NC):
                        output(k, t, c)
                    for j in range(NT if attends else 0):
                        aggregate(ab, i, k, t + 2, j, x_count(i, k + 2), False)
                        if k >= 8 and j in (1, 2, 5, 7) and not last:
                            q = (1, 2, 5, 7).index(j)
                            mask_tile((k % 2) * 4 + q, masks_before(i, k) + q + 1, False)

            with pe.Fori(0, PAIRS - 1) as i:
                pair(i, False)
            pair(PAIRS - 1, True)


_INS = ['x', 'adj', 'L0_gnn_attn_w', 'L0_gnn_attn_b', 'L0_gnn_W1', 'L0_gnn_b1', 'L0_gnn_W2', 'L0_gnn_b2',
        'L0_gnn_g1', 'L0_gnn_beta1', 'L0_gnn_g2', 'L0_gnn_beta2']


def kernel(**inputs):
    import numpy as _np
    import concourse.bacc as _bacc
    from concourse import mybir as _mybir
    from concourse.bass_utils import run_bass_kernel_spmd as _run

    nc = _bacc.Bacc("TRN2", target_bir_lowering=False, num_devices=1)
    arrays, args = {}, []
    for name in _INS:
        a = _np.ascontiguousarray(inputs[name])
        arrays[f"in_{name}_dram"] = a
        args.append(nc.dram_tensor(f"in_{name}_dram", a.shape, _mybir.dt.from_np(a.dtype), kind="ExternalInput").ap())
    out = nc.dram_tensor("out_0_dram", (B, N, D), _mybir.dt.float32, kind="ExternalOutput").ap()
    gnn_kernel(nc, *args, out)
    r = _run(nc, [arrays], core_ids=[0])
    return r.results[0]["out_0_dram"]
```
